# Optimizing a Trainium2 kernel written in Bass

```python
import numpy as np
import jax
import jax.numpy as jnp

def _softmax(x, axis=-1):
    return jax.nn.softmax(x, axis=axis)

def _gelu(x):
    return jax.nn.gelu(x, approximate=True)

def _silu(x):
    return jax.nn.silu(x)

def _sigmoid(x):
    return jax.nn.sigmoid(x)

def _layernorm(x, axis=-1, eps=1e-05):
    m = jnp.mean(x, axis=axis, keepdims=True)
    v = jnp.var(x, axis=axis, keepdims=True)
    return (x - m) / jnp.sqrt(v + eps)

def _scatter_add(tgt, idx, src, axis=0):
    return tgt.at[idx].add(src)

def _segment_sum(src, seg, n):
    return jax.ops.segment_sum(src, seg, n)
kernel_name = 'mk_adj_resnorm_d4_adj_r2_55eff1'

def setup_inputs(seed: int=0):
    np.random.seed(seed)
    _w = jnp.asarray

    def _rec_inputs():
        import jax
        import jax.numpy as jnp
        _gk = jax.random.key(seed)
        x = 7.22e-05 + 1 * jax.random.normal(jax.random.fold_in(_gk, 1), (128, 128, 256), jnp.float32)
        _a = jax.random.bernoulli(jax.random.fold_in(_gk, 2), 0.0625, (128, 128, 128))
        _a = jnp.logical_or(_a, jnp.swapaxes(_a, -1, -2))
        _a = jnp.logical_or(_a, jnp.eye(128, dtype=bool))
        _af = _a.astype(jnp.float32)
        _af = _af * jax.random.uniform(jax.random.fold_in(_gk, 3), (128, 128, 128), jnp.float32, 0.05, 1)
        adj = _af
        return (x, adj)
    x, adj = _rec_inputs()

    def _L0_gnn_setup():
        import jax, jax.numpy as jnp
        import numpy as np
        EPS_LN = 1e-05

        def hypergraph_conv(x, adj, W, b):
            N, C, _ = adj.shape
            H = (adj != 0).astype(x.dtype)
            w = adj.reshape(N, -1)[:, :C]
            xw = jnp.einsum('ncd,hd->nch', x, W)
            Dn = jnp.einsum('nce,ne->nc', H, w)
            Dn = jnp.where(Dn > 0, 1.0 / Dn, 0.0)
            Be = H.sum(axis=1)
            Be = jnp.where(Be > 0, 1.0 / Be, 0.0)
            m = Be[:, :, None] * jnp.einsum('nce,nch->neh', H, xw)
            out = Dn[:, :, None] * jnp.einsum('nce,neh->nch', H, m)
            return out + b

        def layer_norm(x, g, b):
            mu = jnp.mean(x, axis=-1, keepdims=True)
            var = jnp.var(x, axis=-1, keepdims=True)
            return (x - mu) * jax.lax.rsqrt(var + EPS_LN) * g + b
        key = jax.random.key(seed)
        ks = jax.random.split(key, 4)
        N, C, Din, Dh, Dout = (16, 512, 256, 512, 256)
        x = jax.random.normal(ks[0], (N, C, Din), dtype=jnp.float32)
        adj = jax.random.uniform(ks[1], (N, C, C), dtype=jnp.float32, minval=0.1, maxval=1.0)
        W1 = jax.random.normal(ks[2], (Dh, Din), dtype=jnp.float32) * (1.0 / np.sqrt(Din))
        b1 = jnp.zeros((Dh,), dtype=jnp.float32)
        gamma = jnp.ones((Dh,), dtype=jnp.float32)
        beta = jnp.zeros((Dh,), dtype=jnp.float32)
        W2 = jax.random.normal(ks[3], (Dout, Dh), dtype=jnp.float32) * (1.0 / np.sqrt(Dh))
        b2 = jnp.zeros((Dout,), dtype=jnp.float32)
        return {'x': x, 'adj': adj, 'W1': W1, 'b1': b1, 'gamma': gamma, 'beta': beta, 'W2': W2, 'b2': b2}
    _L0_gnn_all = _L0_gnn_setup()
    _L0_gnn_in = {k: v for k, v in _L0_gnn_all.items() if k in ('W1', 'b1', 'gamma', 'beta', 'W2', 'b2')}
    del _L0_gnn_all

    def _L1_gnn_setup():
        import jax, jax.numpy as jnp
        import numpy as np
        EPS = 1e-06
        key = jax.random.key(seed)
        k1, k2, k3 = jax.random.split(key, 3)
        B, N, F, O = (8, 2048, 256, 256)
        x = jax.random.normal(k1, (B, N, F), dtype=jnp.float32)
        adj = jax.random.uniform(k2, (B, N, N), dtype=jnp.float32)
        W = jax.random.normal(k3, (O, 2 * F), dtype=jnp.float32) * (1.0 / np.sqrt(2 * F))
        return {'x': x, 'adj': adj, 'W': W}
    _L1_gnn_all = _L1_gnn_setup()
    _L1_gnn_in = {k: v for k, v in _L1_gnn_all.items() if k in ('W',)}
    del _L1_gnn_all

    def _L2_gnn_setup():
        import jax, jax.numpy as jnp
        import numpy as np
        B, N, F_IN, F_HID, F_OUT = (32, 512, 256, 256, 256)

        def _gcn_layer(x, adj, W, b):
            support = jnp.einsum('bnf,fh->bnh', x, W)
            return jnp.einsum('bnm,bmh->bnh', adj, support) + b
        key = jax.random.key(seed)
        ks = jax.random.split(key, 8)

        def xavier(k, fan_in, fan_out):
            bound = float(np.sqrt(6.0 / (fan_in + fan_out)))
            return jax.random.uniform(k, (fan_in, fan_out), jnp.float32, -bound, bound)
        return {'batch_graph': jax.random.normal(ks[0], (B, N, F_IN), jnp.float32), 'adj': jax.random.uniform(ks[1], (B, N, N), jnp.float32), 'W1': xavier(ks[2], F_IN, F_HID), 'b1': jnp.zeros((F_HID,), jnp.float32), 'W2': xavier(ks[3], F_HID, F_HID), 'b2': jnp.zeros((F_HID,), jnp.float32), 'W3': xavier(ks[4], F_HID, F_OUT), 'b3': jnp.zeros((F_OUT,), jnp.float32)}
    _L2_gnn_all = _L2_gnn_setup()
    _L2_gnn_in = {k: v for k, v in _L2_gnn_all.items() if k in ('W1', 'b1', 'W2', 'b2', 'W3', 'b3')}
    del _L2_gnn_all

    def _L3_gnn_setup():
        import jax, jax.numpy as jnp
        import numpy as np
        key = jax.random.key(seed)
        k1, k2, k3 = jax.random.split(key, 3)
        B, N, F, D = (8, 1024, 256, 256)
        x = jax.random.normal(k1, (B, N, F), dtype=jnp.float32)
        a = jax.random.uniform(k2, (B, N, N), dtype=jnp.float32)
        kernel = jax.random.normal(k3, (F, D), dtype=jnp.float32) * (1.0 / np.sqrt(F))
        return {'x': x, 'a': a, 'kernel': kernel}
    _L3_gnn_all = _L3_gnn_setup()
    _L3_gnn_in = {k: v for k, v in _L3_gnn_all.items() if k in ('kernel',)}
    del _L3_gnn_all
    return {'x': x, 'adj': adj, 'L0_gnn_W1': _L0_gnn_in['W1'], 'L0_gnn_b1': _L0_gnn_in['b1'], 'L0_gnn_gamma': _L0_gnn_in['gamma'], 'L0_gnn_beta': _L0_gnn_in['beta'], 'L0_gnn_W2': _L0_gnn_in['W2'], 'L0_gnn_b2': _L0_gnn_in['b2'], 'L1_gnn_W': _L1_gnn_in['W'], 'L2_gnn_W1': _L2_gnn_in['W1'], 'L2_gnn_b1': _L2_gnn_in['b1'], 'L2_gnn_W2': _L2_gnn_in['W2'], 'L2_gnn_b2': _L2_gnn_in['b2'], 'L2_gnn_W3': _L2_gnn_in['W3'], 'L2_gnn_b3': _L2_gnn_in['b3'], 'L3_gnn_kernel': _L3_gnn_in['kernel']}

def reference(x, adj, L0_gnn_W1, L0_gnn_b1, L0_gnn_gamma, L0_gnn_beta, L0_gnn_W2, L0_gnn_b2, L1_gnn_W, L2_gnn_W1, L2_gnn_b1, L2_gnn_W2, L2_gnn_b2, L2_gnn_W3, L2_gnn_b3, L3_gnn_kernel):
    import jax
    import jax.numpy as jnp

    def _L0_gnn_ref(x, adj, W1, b1, gamma, beta, W2, b2):
        import jax, jax.numpy as jnp
        import numpy as np
        EPS_LN = 1e-05

        def hypergraph_conv(x, adj, W, b):
            N, C, _ = adj.shape
            H = (adj != 0).astype(x.dtype)
            w = adj.reshape(N, -1)[:, :C]
            xw = jnp.einsum('ncd,hd->nch', x, W)
            Dn = jnp.einsum('nce,ne->nc', H, w)
            Dn = jnp.where(Dn > 0, 1.0 / Dn, 0.0)
            Be = H.sum(axis=1)
            Be = jnp.where(Be > 0, 1.0 / Be, 0.0)
            m = Be[:, :, None] * jnp.einsum('nce,nch->neh', H, xw)
            out = Dn[:, :, None] * jnp.einsum('nce,neh->nch', H, m)
            return out + b

        def layer_norm(x, g, b):
            mu = jnp.mean(x, axis=-1, keepdims=True)
            var = jnp.var(x, axis=-1, keepdims=True)
            return (x - mu) * jax.lax.rsqrt(var + EPS_LN) * g + b
        h = jax.nn.relu(hypergraph_conv(x, adj, W1, b1))
        h = layer_norm(h, gamma, beta)
        y = hypergraph_conv(h, adj, W2, b2)
        return y + x

    def _L1_gnn_ref(x, adj, W):
        import jax, jax.numpy as jnp
        import numpy as np
        EPS = 1e-06
        deg = jnp.sum(adj, axis=-1, keepdims=True)
        agg = jnp.einsum('bij,bjf->bif', adj, x) / jnp.maximum(deg, EPS)
        cat = jnp.concatenate([x, agg], axis=2)
        out = jnp.einsum('bnf,of->bno', cat, W)
        return jax.nn.relu(out)

    def _L2_gnn_ref(batch_graph, adj, W1, b1, W2, b2, W3, b3):
        import jax, jax.numpy as jnp
        import numpy as np
        B, N, F_IN, F_HID, F_OUT = (32, 512, 256, 256, 256)

        def _gcn_layer(x, adj, W, b):
            support = jnp.einsum('bnf,fh->bnh', x, W)
            return jnp.einsum('bnm,bmh->bnh', adj, support) + b
        x = jax.nn.relu(_gcn_layer(batch_graph, adj, W1, b1))
        x = jax.nn.relu(_gcn_layer(x, adj, W2, b2))
        out = _gcn_layer(x, adj, W3, b3)
        return out

    def _L3_gnn_ref(x, a, kernel):
        import jax, jax.numpy as jnp
        import numpy as np
        t = jnp.einsum('bnm,bmf->bnf', a, x)
        out = jnp.einsum('bnf,fd->bnd', t, kernel)
        out = jax.nn.relu(out)
        mask = (jnp.sum((x != 0).astype(jnp.float32), axis=-1, keepdims=True) > 0).astype(jnp.float32)
        return out * mask
    x = _layernorm(x + _L0_gnn_ref(x, adj, L0_gnn_W1, L0_gnn_b1, L0_gnn_gamma, L0_gnn_beta, L0_gnn_W2, L0_gnn_b2), axis=-1)
    x = _layernorm(x + _L1_gnn_ref(x, adj, L1_gnn_W), axis=-1)
    x = _layernorm(x + _L2_gnn_ref(x, adj, L2_gnn_W1, L2_gnn_b1, L2_gnn_W2, L2_gnn_b2, L2_gnn_W3, L2_gnn_b3), axis=-1)
    x = _layernorm(x + _L3_gnn_ref(x, adj, L3_gnn_kernel), axis=-1)
    return x

_drawn_inputs = setup_inputs


def setup_inputs(seed=0):
    import zlib

    import numpy as np

    out = dict(_drawn_inputs(seed))
    spreads = {'L0_gnn_b1': (0.0, 0.1),
     'L0_gnn_gamma': (1.0, 0.2),
     'L0_gnn_beta': (0.0, 0.1),
     'L0_gnn_b2': (0.0, 0.343),
     'L2_gnn_b1': (0.0, 0.562),
     'L2_gnn_b2': (0.0, 2.0),
     'L2_gnn_b3': (0.0, 2.0)}
    factors = {}
    for name, (base, spread) in spreads.items():
        noise = np.random.default_rng([zlib.crc32(name.encode()), seed]).standard_normal(out[name].shape)
        drawn = base * np.exp(spread * noise) if base else spread * noise
        out[name] = jnp.asarray(drawn.astype(out[name].dtype))
    for name, factor in factors.items():
        out[name] = (out[name] * factor).astype(out[name].dtype)
    return out
```

```python
from contextlib import ExitStack

import concourse.bass as bass
from concourse import mybir

F32 = mybir.dt.float32
F32R = mybir.dt.float32r
ALU = mybir.AluOpType
ACT = mybir.ActivationFunctionType
AX_X = mybir.AxisListType.X

LN_EPS = 1e-5
DEG_EPS = 1e-6
TINY = 1.1754944e-38

LAG = dict(prep=0, G=0, Tr=0, Gx=0,
           R=1, P=1, GP=1,
           xT=2, XAB=2, AXB=2,
           Ax2=3, H1=3, H1W=3, H2=3,
           H2W=4, AP3=4, Ax3=4, TK=4,
           F=5)
PLACE = dict(R=0, xT=2, H2W=3, Ax2=4, G=5, XAB=6, H1=8, AP3=9, P=10, Tr=12, AXB=13, H1W=14,
             Ax3=15, Gx=16, GP=17, H2=18, TK=19)
PLACES = 20
BANKS = 8
UNROLL = 4
FIRST_IN_LOOP = 8


def build(nc, x, adjT, w1T, w2T, gamma, beta, b1, b2, wT, v1, v2, v3, c1, c2, c3, wk, eye, out):
    NP, C, GP_, D = x.shape
    DH = w1T.shape[2]
    KD, KH = D // C, DH // C
    assert (C, GP_, D, DH) == (128, 2, 256, 512) and NP % UNROLL == 0 and NP > FIRST_IN_LOOP
    END = NP + LAG["F"]

    with ExitStack() as ctx:
        def sb(name, shape, dt=F32):
            return ctx.enter_context(nc.sbuf_tensor(name, [C, *shape], dt))

        def hi_lo(name, shape):
            return [sb(f"{name}_hi", shape, F32R), sb(f"{name}_lo", shape, F32R)]

        def sem(name):
            return ctx.enter_context(nc.semaphore(name))

        psum = ctx.enter_context(nc.psum_tensor("psum", [C, BANKS, 512], F32))

        w2g = sb("w2g", [KH, D])
        w1T_s, w2c_s = hi_lo("w1T", [KD, DH]), hi_lo("w2c", [KH, D + 2])
        wab_s, wk_s = hi_lo("wab", [KD, 2 * D]), hi_lo("wk", [KD, D])
        v_s = [hi_lo(f"v{j}", [KD, D]) for j in range(3)]
        gamma_c, beta_c, b1_c = sb("gamma_c", [KH]), sb("beta_c", [KH]), sb("b1_c", [KH])
        c1_c, c2_c = sb("c1_c", [KD]), sb("c2_c", [KD])
        b2_b, b2half, c3_b = sb("b2_b", [D]), sb("b2half", [D]), sb("c3_b", [D])
        beta_b, w2mean, betaW = sb("beta_b", [KH, C]), sb("w2mean", [D]), sb("betaW", [D])
        ones, ident = sb("ones", [C]), sb("ident", [C])
        ones_r = sb("ones_r", [2], F32R)
        eps_c, wait_pad = sb("eps_c", [1]), sb("wait_pad", [1])

        RING = 4
        x_in = sb("x_in", [RING, 2, D])
        at_in = sb("at_in", [RING, 2, C])
        HT = sb("HT", [2, C], F32R)
        ht_count, be = sb("ht_count", [2]), sb("be", [2])
        be_r, be_parts = sb("be_r", [2], F32R), sb("be_parts", [2, 2])
        BH = sb("BH", [2, 2, C], F32R)
        dn_max, dn_inv, dinv = sb("dn_max", [2]), sb("dn_inv", [2]), sb("dinv", [2])
        Gd = sb("Gd", [2, C])
        GT = [hi_lo(f"GT{b}", [2, C]) for b in range(2)]
        xs = hi_lo("xs", [2, D])
        gx = hi_lo("gx", [KD, 2, C])
        r_f, r_s = sb("r_f", [KH, 2, C]), hi_lo("r", [KH, 2, C])
        sq, sq2, sq1 = sb("sq", [KH, 2, C]), sb("sq2", [2, 2, C]), sb("sq1", [2, C])
        h_mean, h_mean2, h_var = sb("h_mean", [2]), sb("h_mean2", [2]), sb("h_var", [2])
        h_veps, h_std, h_rstd = sb("h_veps", [2]), sb("h_std", [2]), sb("h_rstd", [2])
        p_f, p_s = sb("p_f", [2, D]), hi_lo("p", [2, D])
        xb = sb("xb", [2, D])
        A = [hi_lo(f"A{b}", [2, C]) for b in range(RING)]
        degm, rdeg = sb("degm", [2]), [sb(f"rdeg{b}", [2]) for b in range(2)]
        x1 = sb("x1", [2, D])
        x1T = hi_lo("x1T", [KD, 2, C])
        xa, xbw, agg = sb("xa", [2, D]), hi_lo("xbw", [2, D]), sb("agg", [2, D])
        x2, x2c = sb("x2", [2, D]), [sb(f"x2c{b}", [2, D]) for b in range(2)]
        x2s = hi_lo("x2s", [2, D])
        ax2 = hi_lo("ax2", [KD, 2, C])
        h1_f, h1_s, h1w = sb("h1_f", [KD, 2, C]), hi_lo("h1", [KD, 2, C]), hi_lo("h1w", [2, D])
        h2_f, h2_s, h2w = sb("h2_f", [KD, 2, C]), hi_lo("h2", [KD, 2, C]), hi_lo("h2w", [2, D])
        x3, x3s = sb("x3", [2, D]), hi_lo("x3s", [2, D])
        nz, nz_count, mask = sb("nz", [2, D]), sb("nz_count", [2]), sb("mask", [2])
        ax3 = hi_lo("ax3", [KD, 2, C])
        tk = sb("tk", [2, D])
        x4 = [sb(f"x4{b}", [2, D]) for b in range(2)]
        w1T_f = r_f[:].rearrange("p (k a) g c -> p k (a g c)", k=KD)
        w2T_f = sq[:].rearrange("p m g c -> p m (g c)")
        wab_f = [h1_f[:].rearrange("p m g c -> p (m g c)"), h2_f[:].rearrange("p m g c -> p (m g c)")]
        v_f, wk_f = [xa[:], agg[:], x2[:]], tk[:]
        class Norm:
            def __init__(self, name):
                self.s = sb(f"{name}_s", [2, D])
                self.st, self.mv = sb(f"{name}_st", [2, 6]), sb(f"{name}_mv", [2, 2])
                self.std, self.rstd = sb(f"{name}_std", [2]), sb(f"{name}_rstd", [2])
                self.summed, self.stats = sem(f"{name}_summed"), sem(f"{name}_stats")
                self.varied, self.rooted = sem(f"{name}_varied"), sem(f"{name}_rooted")
                self.inverted, self.done = sem(f"{name}_inverted"), sem(f"{name}_done")
        n1, n2, n3, n4 = Norm("n1"), Norm("n2"), Norm("n3"), Norm("n4")

        load_w, w_prep_step, w_prep, w_ps, w_ready = (
            sem(s) for s in ("load_w", "w_prep_step", "w_prep", "w_ps", "w_ready"))
        x_loaded, at_loaded = ([sem(f"{name}_loaded{j}") for j in range(RING)] for name in ("x", "at"))
        stored = [sem(f"stored{j}") for j in range(2)]
        pe_did = {s: sem(f"pe_{s}") for s in PLACE}
        pe_R0 = sem("pe_R0")
        ht_made, ht_counted, be_max, be_made, be_hi, be_lo, bh_made = (
            sem(s) for s in ("ht_made", "ht_counted", "be_max", "be_made", "be_hi", "be_lo", "bh_made"))
        dn_1, dn_2, dn_3, gd_made = sem("dn_1"), sem("dn_2"), sem("dn_3"), sem("gd_made")
        gt_hi, gt_lo = sem("gt_hi"), sem("gt_lo")
        xs_hi, xs_lo, gx_hi, gx_lo = sem("xs_hi"), sem("xs_lo"), sem("gx_hi"), sem("gx_lo")
        r_relu, r_hi = [sem(f"r_relu{j}") for j in range(2)], [sem(f"r_hi{j}") for j in range(2)]
        r_lo, sq_made, sq_half, sq_sum = sem("r_lo"), sem("sq_made"), sem("sq_half"), sem("sq_sum")
        hm, hm2, hv, hve, hstd, hrstd = (sem(f"h_stat{j}") for j in range(6))
        deg_max, deg_inv = sem("deg_max"), sem("deg_inv")
        p_made, p_hi, p_lo, xb_made = sem("p_made"), sem("p_hi"), sem("p_lo"), sem("xb_made")
        a_hi, a_lo = sem("a_hi"), sem("a_lo")
        x1T_hi, x1T_lo = sem("x1T_hi"), sem("x1T_lo")
        xa_out, xbw_hi, xbw_lo = sem("xa_out"), sem("xbw_hi"), sem("xbw_lo")
        agg_made = sem("agg_made")
        x2_hi, x2_lo, x2c_made = sem("x2_hi"), sem("x2_lo"), sem("x2c_made")
        ax2_hi, ax2_lo = sem("ax2_hi"), sem("ax2_lo")
        h1_relu, h1_hi, h1_lo, h1w_hi, h1w_lo = (sem(s) for s in ("h1_relu", "h1_hi", "h1_lo", "h1w_hi", "h1w_lo"))
        h2_relu, h2_hi, h2_lo, h2w_hi, h2w_lo = (sem(s) for s in ("h2_relu", "h2_hi", "h2_lo", "h2w_hi", "h2w_lo"))
        x3_hi, x3_lo, x3_nz, mask_made = sem("x3_hi"), sem("x3_lo"), sem("x3_nz"), sem("mask_made")
        ax3_hi, ax3_lo, tk_relu = sem("ax3_hi"), sem("ax3_lo"), sem("tk_relu")

        def begun(pair):
            return not isinstance(pair, int) or pair >= 0

        def upto(pair):
            return min(pair, NP - 1) + 1 if isinstance(pair, int) else pair + 1

        def active(stage, n):
            return not isinstance(n, int) or 0 <= n - LAG[stage] < NP

        def bank(stage, k, extra=0):
            return (PLACES * k + PLACE[stage] + extra) % BANKS

        def steps(eng, body, ahead=0):
            stop = NP if not ahead else NP - UNROLL
            for n in range(FIRST_IN_LOOP):
                body(n, n)
            with eng.Fori(FIRST_IN_LOOP, stop - UNROLL + 1, UNROLL) as base:
                for k in range(UNROLL):
                    body(base + k, k)
            for n in range(stop, END):
                body(n, n)

        def at_count(p, k):
            if isinstance(p, int):
                return 16 * (p // RING + 1)
            return (p + (RING - k % RING)) * (16 // RING)

        def f(ap):
            return ap.bitcast(F32)

        def bc(ap, shape, axis):
            return ap.unsqueeze(axis).to_broadcast(shape)

        block = ctx.enter_context(nc.Block())

        @block.sync
        def _(sp):
            wTk = wT.rearrange("(h k p) d -> h p k d", h=2, p=C)
            for dst, src in (
                (w1T_f, w1T), (w2T_f, w2T), (gamma_c[:], gamma), (beta_c[:], beta), (b1_c[:], b1),
                *((wab_f[kk][:, h * D:(h + 1) * D], wTk[h, :, kk]) for h in range(2) for kk in range(KD)),
                (v_f[0], v1), (v_f[1], v2), (v_f[2], v3), (wk_f, wk),
                (c1_c[:], c1), (c2_c[:], c2), (ident[:], eye),
                (b2_b[:], b2.partition_broadcast(C)), (c3_b[:], c3.partition_broadcast(C)),
            ):
                sp.dma_start(dst, src).then_inc(load_w, 16)

            def load(pair, k):
                sp.dma_start(at_in[:, k % RING], adjT[pair]).then_inc(at_loaded[k % RING], 16)
                sp.dma_start(x_in[:, k % RING], x[pair]).then_inc(x_loaded[k % RING], 16)

            load(0, 0)
            load(1, 1)

            def body(n, k):
                if not isinstance(n, int) or n + 2 < NP:
                    if begun(n - 2):
                        sp.wait_ge(xs_lo, upto(n - 2))
                    if begun(n - 2):
                        sp.wait_ge(xb_made, upto(n - 2))
                    if begun(n - 2):
                        sp.wait_ge(pe_did["G"], upto(n - 2))
                    if begun(n - 2):
                        sp.wait_ge(a_lo, upto(n - 2))
                    if isinstance(n, int):
                        load(n + 2, k + 2)
                    else:
                        sp.dma_start(at_in[:, (k + 2) % RING],
                                     adjT[bass.ds(n + 2, 1)].rearrange("a p g c -> p (a g) c")
                                     ).then_inc(at_loaded[(k + 2) % RING], 16)
                        sp.dma_start(x_in[:, (k + 2) % RING],
                                     x[bass.ds(n + 2, 1)].rearrange("a p g c -> p (a g) c")
                                     ).then_inc(x_loaded[(k + 2) % RING], 16)
                if active("F", n):
                    p = n - LAG["F"]
                    sp.wait_ge(n4.done, upto(p))
                    src = x4[(k - LAG["F"]) % 2]
                    if isinstance(p, int):
                        sp.dma_start(out[p], src[:]).then_inc(stored[(k - 5) % 2], 16)
                    else:
                        sp.dma_start(out[bass.ds(p, 1)].rearrange("a p g c -> p (a g) c"),
                                     src[:]).then_inc(stored[(k - 5) % 2], 16)

            steps(sp, body, ahead=2)
            for j in range(2):
                sp.wait_ge(stored[j], 16 * NP // 2)

        @block.tensor
        def _(pe):
            def mm(o, a, b, start, stop):
                return pe.matmul(o, a, b, start=start, stop=stop)

            def product(o, terms):
                last = None
                for t, (a, b) in enumerate(terms):
                    last = mm(o, a[0], b[0], t == 0, False)
                    mm(o, a[0], b[1], False, False)
                    last = mm(o, a[1], b[0], False, t == len(terms) - 1)
                return last

            def part(s, *idx):
                return [s[0][idx], s[1][idx]]

            ALL = slice(None)

            def cols(m):
                return slice(m * C, (m + 1) * C)

            pe.wait_ge(load_w, 16 * 18)
            pe.wait_ge(w_prep, 1)
            for m in range(KH):
                mm(psum[:, 0, 0:D], ones[:], w2g[:, m, :], m == 0, m == KH - 1)
            for m in range(KH):
                last = mm(psum[:, 1, 0:D], beta_b[:, m, :], w2T_f[:, m, :], m == 0, m == KH - 1)
            last.then_inc(w_ps, 1)
            pe.wait_ge(w_ready, 1)

            def propagate_T(stage, k, state, adj, p, waits):
                b = bank(stage, k)
                for m in range(KD):
                    for g in range(2):
                        last = product(psum[:, b, (2 * m + g) * C:(2 * m + g + 1) * C],
                                       [(part(state, ALL, g, cols(m)), part(adj, ALL, g))])
                last.then_inc(pe_did[stage], 1)

            def propagate(stage, k, adj, state):
                b = bank(stage, k)
                for g in range(2):
                    last = product(psum[:, b, g * D:(g + 1) * D],
                                   [(part(adj, ALL, g), part(state, ALL, g))])
                last.then_inc(pe_did[stage], 1)

            def weigh(stage, k, stateT, w):
                b = bank(stage, k)
                for g in range(2):
                    last = product(psum[:, b, g * D:(g + 1) * D],
                                   [(part(stateT, ALL, m, g), part(w, ALL, m)) for m in range(KD)])
                last.then_inc(pe_did[stage], 1)

            def body(n, k):
                if active("R", n):
                    p = n - 1
                    pe.wait_ge(gx_hi, upto(p))
                    pe.wait_ge(gx_lo, upto(p))
                    for m in range(KH):
                        if m == 0:
                            if begun(n - 1):
                                pe.wait_ge(gt_lo, upto(n - 1))
                        if m == 2:
                            if begun(n - 3):
                                pe.wait_ge(agg_made, upto(n - 3))
                        o = psum[:, bank("R", k, m // 2), (m % 2) * 2 * C:(m % 2 + 1) * 2 * C]
                        last = product(o, [(part(w1T_s, ALL, kk, cols(m)), part(gx, ALL, kk))
                                           for kk in range(KD)])
                        if m == 1:
                            last.then_inc(pe_R0, 1)
                    last.then_inc(pe_did["R"], 1)
                if active("xT", n):
                    p = n - 2
                    pe.wait_ge(n1.done, upto(p))
                    if begun(n - 4):
                        pe.wait_ge(h1w_lo, upto(n - 4))
                    for m in range(KD):
                        for g in range(2):
                            last = pe.transpose(psum[:, bank("xT", k), (2 * m + g) * C:(2 * m + g + 1) * C],
                                                x1[:, g, cols(m)], ident[:])
                    last.then_inc(pe_did["xT"], 1)
                if active("H2W", n):
                    p = n - 4
                    pe.wait_ge(h2_hi, upto(p))
                    pe.wait_ge(h2_lo, upto(p))
                    if begun(n - 5):
                        pe.wait_ge(ax3_lo, upto(n - 5))
                    weigh("H2W", k, h2_s, v_s[2])
                if active("Ax2", n):
                    p = n - 3
                    pe.wait_ge(x2_hi, upto(p))
                    pe.wait_ge(x2_lo, upto(p))
                    if begun(n - 1):
                        pe.wait_ge(gx_lo, upto(n - 1))
                    propagate_T("Ax2", k, x2s, A[(k - 3) % RING], p, None)
                if active("G", n):
                    p = n
                    pe.wait_ge(bh_made, upto(p))
                    pe_at = at_in[:, k % RING]
                    if begun(n - 2):
                        pe.wait_ge(n1.summed, upto(n - 2))
                    b = bank("G", k)
                    pe.wait_ge(at_loaded[k % RING], at_count(p, k))
                    for g in range(2):
                        mm(psum[:, b, cols(g)], HT[:, g, :], BH[:, 0, g, :], True, False)
                        mm(psum[:, b, cols(g)], HT[:, g, :], BH[:, 1, g, :], False, True)
                    for g in range(2):
                        last = mm(psum[:, b, 2 * C + g:2 * C + g + 1], f(HT[:, g, :]),
                                  at_in[:, k % RING, g, 0:1], True, True)
                    last.then_inc(pe_did["G"], 1)
                if active("XAB", n):
                    p = n - 2
                    pe.wait_ge(x1T_hi, upto(p))
                    pe.wait_ge(x1T_lo, upto(p))
                    if begun(n - 4):
                        pe.wait_ge(h2_relu, upto(n - 4))
                    if begun(n - 5):
                        pe.wait_ge(tk_relu, upto(n - 5))
                    for g in range(2):
                        last = product(psum[:, bank("XAB", k, g), :],
                                       [(part(x1T, ALL, m, g), part(wab_s, ALL, m)) for m in range(KD)])
                    last.then_inc(pe_did["XAB"], 1)
                if active("H1", n):
                    p = n - 3
                    pe.wait_ge(ax2_hi, upto(p))
                    pe.wait_ge(ax2_lo, upto(p))
                    if begun(n - 1):
                        pe.wait_ge(r_relu[0], upto(n - 1))
                    for m in range(KD):
                        last = product(psum[:, bank("H1", k), m * 2 * C:(m + 1) * 2 * C],
                                       [(part(v_s[0], ALL, kk, cols(m)), part(ax2, ALL, kk)) for kk in range(KD)])
                    last.then_inc(pe_did["H1"], 1)
                if active("AP3", n):
                    p = n - 4
                    pe.wait_ge(h2w_hi, upto(p))
                    pe.wait_ge(h2w_lo, upto(p))
                    if begun(n - 1):
                        pe.wait_ge(r_relu[1], upto(n - 1))
                    propagate("AP3", k, A[(k - 4) % RING], h2w)
                if active("P", n):
                    p = n - 1
                    pe.wait_ge(r_hi[0], upto(p))
                    pe.wait_ge(r_hi[1], upto(p))
                    pe.wait_ge(r_lo, upto(p))
                    pe.wait_ge(sq_sum, upto(p))
                    pe.wait_ge(a_hi, upto(p))
                    pe.wait_ge(a_lo, upto(p))
                    if begun(n - 2):
                        pe.wait_ge(x1T_lo, upto(n - 2))
                    if begun(n - 4):
                        pe.wait_ge(h2w_lo, upto(n - 4))
                    adj = A[(k - 1) % RING]
                    for g in range(2):
                        b = bank("P", k, g)
                        product(psum[:, b, 0:D + 2],
                                [(part(r_s, ALL, m, g), part(w2c_s, ALL, m)) for m in range(KH)])
                        mm(psum[:, b, D + 2:D + 3], sq1[:, g, :], ones[:, 0:1], True, True)
                        mm(psum[:, b, D + 4:D + 6], adj[0][:, g, :], ones_r[:], True, False)
                        last = mm(psum[:, b, D + 4:D + 6], adj[1][:, g, :], ones_r[:], False, True)
                    last.then_inc(pe_did["P"], 1)
                if active("Tr", n):
                    p = n
                    pe.wait_ge(gd_made, upto(p))
                    if begun(n - 3):
                        pe.wait_ge(ax2_lo, upto(n - 3))
                    for g in range(2):
                        last = pe.transpose(psum[:, bank("Tr", k), cols(g)], Gd[:, g, :], ident[:])
                    last.then_inc(pe_did["Tr"], 1)
                if active("AXB", n):
                    p = n - 2
                    pe.wait_ge(xbw_hi, upto(p))
                    pe.wait_ge(xbw_lo, upto(p))
                    pe.wait_ge(gd_made, upto(n))
                    propagate("AXB", k, A[(k - 2) % RING], xbw)
                if active("H1W", n):
                    p = n - 3
                    pe.wait_ge(h1_hi, upto(p))
                    pe.wait_ge(h1_lo, upto(p))
                    if begun(n - 2):
                        pe.wait_ge(xbw_lo, upto(n - 2))
                    weigh("H1W", k, h1_s, v_s[1])
                if active("Ax3", n):
                    p = n - 4
                    pe.wait_ge(x3_hi, upto(p))
                    pe.wait_ge(x3_lo, upto(p))
                    if begun(n - 2):
                        pe.wait_ge(xbw_lo, upto(n - 2))
                    propagate_T("Ax3", k, x3s, A[(k - 4) % RING], p, None)
                if active("Gx", n):
                    p = n
                    pe.wait_ge(gt_hi, upto(p))
                    pe.wait_ge(gt_lo, upto(p))
                    pe.wait_ge(xs_hi, upto(p))
                    pe.wait_ge(xs_lo, upto(p))
                    if begun(n - 3):
                        pe.wait_ge(h1_relu, upto(n - 3))
                    propagate_T("Gx", k, xs, GT[k % 2], p, None)
                if active("GP", n):
                    p = n - 1
                    pe.wait_ge(p_hi, upto(p))
                    pe.wait_ge(p_lo, upto(p))
                    if begun(n - 4):
                        pe.wait_ge(n3.summed, upto(n - 4))
                    propagate("GP", k, GT[(k - 1) % 2], p_s)
                if active("H2", n):
                    p = n - 3
                    pe.wait_ge(h1w_hi, upto(p))
                    pe.wait_ge(h1w_lo, upto(p))
                    if begun(n - 1):
                        pe.wait_ge(p_made, upto(n - 1))
                    propagate_T("H2", k, h1w, A[(k - 3) % RING], p, None)
                if active("TK", n):
                    p = n - 4
                    pe.wait_ge(ax3_hi, upto(p))
                    pe.wait_ge(ax3_lo, upto(p))
                    if begun(n - 1):
                        pe.wait_ge(p_made, upto(n - 1))
                    weigh("TK", k, ax3, wk_s)

            steps(pe, body)

        @block.scalar
        def _(act):
            def copy(o, i):
                return act.activation(o, i, ACT.Copy)

            def split_hi(stage, n, k, dst, signal, p, used):
                act.wait_ge(pe_did[stage], upto(p))
                if begun(p - 1):
                    act.wait_ge(used, upto(p - 1))
                copy(dst[0][:].rearrange("p a b -> p (a b)") if len(dst[0].shape) == 3 else
                     dst[0][:].rearrange("p a b c -> p (a b c)"),
                     psum[:, bank(stage, k), 0:2 * D]).then_inc(signal, 1)

            def root(nm, p):
                act.wait_ge(nm.varied, upto(p))
                if begun(p - 1):
                    act.wait_ge(nm.inverted, upto(p - 1))
                act.activation(nm.std[:], nm.mv[:, :, 1], ACT.Sqrt, bias=eps_c[:, 0:1]).then_inc(nm.rooted, 1)

            act.wait_ge(w_ready, 1)

            def body(n, k):
                if active("prep", n):
                    act.wait_ge(x_loaded[k % RING], at_count(n, k))
                    if begun(n - 1):
                        act.wait_ge(pe_did["Gx"], upto(n - 1))
                    copy(xs[0][:], x_in[:, k % RING]).then_inc(xs_hi, 1)
                if active("R", n):
                    p = n - 1
                    for m in range(KH):
                        if m == 0:
                            act.wait_ge(pe_R0, upto(p))
                            if begun(p - 1):
                                act.wait_ge(sq_made, upto(p - 1))
                            if begun(p - 1):
                                act.wait_ge(r_lo, upto(p - 1))
                            if begun(p - 1):
                                act.wait_ge(r_hi[1], upto(p - 1))
                        if m == 2:
                            act.wait_ge(pe_did["R"], upto(p))
                        last = act.activation(
                            r_f[:, m].rearrange("p g c -> p (g c)"),
                            psum[:, bank("R", k, m // 2), (m % 2) * 2 * C:(m % 2 + 1) * 2 * C],
                            ACT.Relu, bias=b1_c[:, m:m + 1])
                        if m % 2:
                            last.then_inc(r_relu[m // 2], 1)
                if active("F", n):
                    root(n4, n - 5)
                if active("xT", n):
                    split_hi("xT", n, k, x1T, x1T_hi, n - 2, pe_did["XAB"])
                if active("H2W", n):
                    split_hi("H2W", n, k, h2w, h2w_hi, n - 4, pe_did["AP3"])
                if active("Ax2", n):
                    split_hi("Ax2", n, k, ax2, ax2_hi, n - 3, pe_did["H1"])
                if active("R", n):
                    p = n - 1
                    act.wait_ge(r_relu[1], upto(p))
                    if begun(p - 1):
                        act.wait_ge(sq_half, upto(p - 1))
                    act.activation(sq[:], r_f[:], ACT.Square).then_inc(sq_made, 1)
                    act.wait_ge(at_loaded[(k - 1) % RING], at_count(p, k - 1))
                    if begun(n - 5):
                        act.wait_ge(pe_did["Ax3"], upto(n - 5))
                    copy(A[(k - 1) % RING][0][:], at_in[:, (k - 1) % RING]).then_inc(a_hi, 1)
                if active("XAB", n):
                    p = n - 2
                    act.wait_ge(pe_did["XAB"], upto(p))
                    if begun(p - 1):
                        act.wait_ge(pe_did["AXB"], upto(p - 1))
                    b = bank("XAB", k)
                    copy(xbw[0][:], psum[:, b:b + 2, D:2 * D]).then_inc(xbw_hi, 1)
                    if begun(p - 1):
                        act.wait_ge(agg_made, upto(p - 1))
                    copy(xa[:], psum[:, b:b + 2, 0:D]).then_inc(xa_out, 1)
                if active("H1", n):
                    p = n - 3
                    act.wait_ge(pe_did["H1"], upto(p))
                    if begun(p - 1):
                        act.wait_ge(h1_lo, upto(p - 1))
                    for m in range(KD):
                        last = act.activation(h1_f[:, m].rearrange("p g c -> p (g c)"),
                                              psum[:, bank("H1", k), m * 2 * C:(m + 1) * 2 * C],
                                              ACT.Relu, bias=c1_c[:, m:m + 1])
                    last.then_inc(h1_relu, 1)
                if active("AP3", n):
                    root(n3, n - 4)
                    if begun(n - 4):
                        act.wait_ge(n3.done, upto(n - 4))
                    if begun(n - 5):
                        act.wait_ge(pe_did["Ax3"], upto(n - 5))
                    copy(x3s[0][:], x3[:]).then_inc(x3_hi, 1)
                if active("P", n):
                    p = n - 1
                    act.wait_ge(hve, upto(p))
                    if begun(p - 1):
                        act.wait_ge(hrstd, upto(p - 1))
                    act.activation(h_std[:], h_veps[:], ACT.Sqrt).then_inc(hstd, 1)
                if active("Tr", n):
                    p = n
                    act.wait_ge(pe_did["Tr"], upto(p))
                    if begun(p - 2):
                        act.wait_ge(pe_did["GP"], upto(p - 2))
                    copy(GT[k % 2][0][:].rearrange("p a b -> p (a b)"),
                         psum[:, bank("Tr", k), 0:2 * C]).then_inc(gt_hi, 1)
                if active("P", n):
                    p = n - 1
                    act.wait_ge(p_made, upto(p))
                    if begun(p - 1):
                        act.wait_ge(pe_did["GP"], upto(p - 1))
                    copy(p_s[0][:], p_f[:]).then_inc(p_hi, 1)
                if active("AXB", n):
                    root(n2, n - 2)
                if active("H1W", n):
                    split_hi("H1W", n, k, h1w, h1w_hi, n - 3, pe_did["H2"])
                if active("AXB", n):
                    if begun(n - 2):
                        act.wait_ge(n2.done, upto(n - 2))
                    if begun(n - 3):
                        act.wait_ge(pe_did["Ax2"], upto(n - 3))
                    copy(x2s[0][:], x2[:]).then_inc(x2_hi, 1)
                if active("Ax3", n):
                    split_hi("Ax3", n, k, ax3, ax3_hi, n - 4, pe_did["TK"])
                if active("Gx", n):
                    split_hi("Gx", n, k, gx, gx_hi, n, pe_did["R"])
                if active("GP", n):
                    root(n1, n - 1)
                if active("H2", n):
                    p = n - 3
                    act.wait_ge(pe_did["H2"], upto(p))
                    if begun(p - 1):
                        act.wait_ge(h2_lo, upto(p - 1))
                    for m in range(KD):
                        last = act.activation(h2_f[:, m].rearrange("p g c -> p (g c)"),
                                              psum[:, bank("H2", k), m * 2 * C:(m + 1) * 2 * C],
                                              ACT.Relu, bias=c2_c[:, m:m + 1])
                    last.then_inc(h2_relu, 1)
                if active("TK", n):
                    p = n - 4
                    act.wait_ge(pe_did["TK"], upto(p))
                    act.wait_ge(mask_made, upto(p))
                    if begun(p - 1):
                        act.wait_ge(n4.summed, upto(p - 1))
                    for g in range(2):
                        last = act.activation(tk[:, g, :], psum[:, bank("TK", k), g * D:(g + 1) * D],
                                              ACT.Relu, scale=mask[:, g:g + 1])
                    last.then_inc(tk_relu, 1)

            steps(act, body)

        @block.vector
        def _(dve):
            def split_lo(dst, src, signal):
                return dve.tensor_tensor(dst[1][:], src, f(dst[0][:]), ALU.subtract).then_inc(signal, 1)

            chain = [0]

            def setup(ins):
                chain[0] += 1
                ins.then_inc(w_prep_step, 1)
                dve.wait_ge(w_prep_step, chain[0])

            dve.wait_ge(load_w, 16 * 18)
            dve.memset(ones[:], 1.0)
            dve.memset(eps_c[:], LN_EPS)
            setup(dve.tensor_scalar(b2half[:], b2_b[:], 0.5, None, ALU.mult))
            for m in range(KH):
                setup(dve.tensor_scalar(w2g[:, m, :], w2T_f[:, m, :], gamma_c[:, m:m + 1], None, ALU.mult))
                setup(dve.tensor_scalar(beta_b[:, m, :], ones[:], beta_c[:, m:m + 1], None, ALU.mult))
            setup(dve.tensor_copy(ones_r[:], ones[:, 0:2]))
            dve.nop().then_inc(w_prep, 1)
            for (hi, lo), src in (
                ([s[:] for s in w1T_s], w1T_f), ([s[:, 0] for s in wab_s], wab_f[0]),
                ([s[:, 1] for s in wab_s], wab_f[1]), ([s[:] for s in wk_s], wk_f),
                *(([s[:] for s in v_s[j]], v_f[j]) for j in range(3)),
            ):
                setup(dve.tensor_copy(hi, src))
                setup(dve.tensor_tensor(lo, src, f(hi), ALU.subtract))
            dve.wait_ge(w_ps, 1)
            setup(dve.tensor_scalar(w2mean[:], psum[:, 0, 0:D], 1.0 / DH, None, ALU.mult))
            setup(dve.tensor_copy(betaW[:], psum[:, 1, 0:D]))
            setup(dve.tensor_tensor(w2T_f, w2g[:], bc(w2mean[:], [C, KH, D], 1), ALU.subtract))
            hi, lo = w2c_s
            setup(dve.tensor_copy(hi[:, :, 0:D], w2T_f))
            setup(dve.tensor_tensor(lo[:, :, 0:D], w2T_f, f(hi[:, :, 0:D]), ALU.subtract))
            setup(dve.tensor_copy(hi[:, :, D:D + 1], ones[:, 0:KH].unsqueeze(2)))
            setup(dve.tensor_scalar(hi[:, :, D + 1:D + 2], ones[:, 0:KH].unsqueeze(2), 0.0, None, ALU.mult))
            setup(dve.tensor_scalar(lo[:, :, D:D + 2], ones[:, 0:2 * KH].rearrange("p (a b) -> p a b", a=KH),
                                    0.0, None, ALU.mult))
            dve.nop().then_inc(w_ready, 1)

            def stats(nm, p):
                dve.wait_ge(nm.summed, upto(p))
                for g in range(2):
                    last = dve.bn_stats(nm.st[:, g, :], nm.s[:, g, :])
                last.then_inc(nm.stats, 1)
                dve.wait_ge(nm.stats, upto(p))
                if begun(p - 1):
                    dve.wait_ge(nm.rooted, upto(p - 1))
                dve.memset(wait_pad[:], 0.0)
                for g in range(2):
                    last = dve.bn_aggr(nm.mv[:, g, :], nm.st[:, g, :])
                last.then_inc(nm.varied, 1)

            def apply(nm, p, dst):
                dve.wait_ge(nm.rooted, upto(p))
                dve.reciprocal(nm.rstd[:], nm.std[:]).then_inc(nm.inverted, 1)
                dve.wait_ge(nm.inverted, upto(p))
                for g in range(2):
                    last = dve.tensor_scalar(dst[:, g, :], nm.s[:, g, :], nm.mv[:, g, 0:1], nm.rstd[:, g:g + 1],
                                             ALU.subtract, ALU.mult)
                last.then_inc(nm.done, 1)

            def flat(b, w=2 * D):
                return psum[:, b, 0:w]

            def body(n, k):
                if active("prep", n):
                    dve.wait_ge(at_loaded[k % RING], at_count(n, k))
                    if begun(n - 1):
                        dve.wait_ge(pe_did["G"], upto(n - 1))
                    dve.tensor_scalar(HT[:], at_in[:, k % RING], 0.0, None, ALU.not_equal).then_inc(ht_made, 1)
                    dve.wait_ge(ht_made, upto(n))
                    dve.tensor_reduce(ht_count[:], f(HT[:]), AX_X, ALU.add).then_inc(ht_counted, 1)
                    dve.wait_ge(ht_counted, upto(n))
                    dve.tensor_scalar(be[:], ht_count[:], 1.0, None, ALU.max).then_inc(be_max, 1)
                    dve.wait_ge(be_max, upto(n))
                    if begun(n - 1):
                        dve.wait_ge(bh_made, upto(n - 1))
                    dve.reciprocal(be_parts[:, 1, :], be[:]).then_inc(be_made, 1)
                    dve.wait_ge(be_made, upto(n))
                    dve.tensor_copy(be_r[:], be_parts[:, 1, :]).then_inc(be_hi, 1)
                    dve.wait_ge(be_hi, upto(n))
                    dve.tensor_copy(be_parts[:, 0, :], f(be_r[:]))
                    dve.tensor_tensor(be_parts[:, 1, :], be_parts[:, 1, :], f(be_r[:]),
                                      ALU.subtract).then_inc(be_lo, 1)
                if active("F", n):
                    p = n - 5
                    dve.wait_ge(tk_relu, upto(p))
                    dve.tensor_tensor(n4.s[:], tk[:], x3[:], ALU.add).then_inc(n4.summed, 1)
                    stats(n4, p)
                if active("R", n):
                    p = n - 1
                    dve.wait_ge(r_relu[0], upto(p))
                    if begun(p - 1):
                        dve.wait_ge(pe_did["P"], upto(p - 1))
                    dve.tensor_copy(r_s[0][:, 0:2], r_f[:, 0:2]).then_inc(r_hi[0], 1)
                if active("F", n):
                    p = n - 5
                    if not isinstance(p, int):
                        dve.wait_ge(stored[(k - 5) % 2], (p - (k - 5) % 2) * 8)
                    elif p >= 2:
                        dve.wait_ge(stored[p % 2], 16 * (p // 2))
                    apply(n4, p, x4[(k - 5) % 2])
                if active("R", n):
                    p = n - 1
                    dve.wait_ge(r_relu[1], upto(p))
                    dve.tensor_copy(r_s[0][:, 2:4], r_f[:, 2:4]).then_inc(r_hi[1], 1)
                if active("xT", n):
                    if begun(n - 2):
                        dve.wait_ge(x1T_hi, upto(n - 2))
                    split_lo(x1T, flat(bank("xT", k)), x1T_lo)
                if active("H2W", n):
                    if begun(n - 4):
                        dve.wait_ge(h2w_hi, upto(n - 4))
                    split_lo(h2w, flat(bank("H2W", k)), h2w_lo)
                if active("Ax2", n):
                    if begun(n - 3):
                        dve.wait_ge(ax2_hi, upto(n - 3))
                    split_lo(ax2, flat(bank("Ax2", k)), ax2_lo)
                if active("G", n):
                    b = bank("G", k)
                    dn = psum[:, b, 2 * C:2 * C + 2]
                    dve.wait_ge(pe_did["G"], upto(n))
                    dve.tensor_scalar(dn_max[:], dn, TINY, None, ALU.max).then_inc(dn_1, 1)
                    dve.wait_ge(dn_1, upto(n))
                    dve.reciprocal(dn_inv[:], dn_max[:]).then_inc(dn_2, 1)
                    dve.wait_ge(dn_2, upto(n))
                    dve.scalar_tensor_tensor(out=dinv[:], in0=dn, scalar=0.0, in1=dn_inv[:],
                                             op0=ALU.is_gt, op1=ALU.mult).then_inc(dn_3, 1)
                    dve.wait_ge(dn_3, upto(n))
                    if begun(n - 1):
                        dve.wait_ge(pe_did["Tr"], upto(n - 1))
                    dve.tensor_tensor(Gd[:], psum[:, b, 0:2 * C].rearrange("p (g c) -> p g c", g=2),
                                      bc(dinv[:], [C, 2, C], 2), ALU.mult).then_inc(gd_made, 1)
                if active("XAB", n):
                    p = n - 2
                    b = bank("XAB", k)
                    dve.wait_ge(xbw_hi, upto(p))
                    dve.wait_ge(xa_out, upto(p))
                    split_lo(xbw, psum[:, b:b + 2, D:2 * D], xbw_lo)
                if active("H1", n):
                    p = n - 3
                    dve.wait_ge(h1_relu, upto(p))
                    if begun(p - 1):
                        dve.wait_ge(pe_did["H1W"], upto(p - 1))
                    dve.tensor_copy(h1_s[0][:], h1_f[:]).then_inc(h1_hi, 1)
                if active("AP3", n):
                    p = n - 4
                    dve.wait_ge(pe_did["AP3"], upto(p))
                    dve.wait_ge(x2c_made, upto(p))
                    dve.tensor_tensor(n3.s[:].rearrange("p g d -> p (g d)"), flat(bank("AP3", k)),
                                      x2c[(k - 4) % 2][:].rearrange("p g d -> p (g d)"),
                                      ALU.add).then_inc(n3.summed, 1)
                    stats(n3, p)
                    if begun(p - 1):
                        dve.wait_ge(n4.summed, upto(p - 1))
                    if begun(p - 1):
                        dve.wait_ge(x3_lo, upto(p - 1))
                    apply(n3, p, x3)
                if active("P", n):
                    p = n - 1
                    b = bank("P", k)
                    dve.wait_ge(pe_did["P"], upto(p))
                    dve.tensor_scalar(h_mean[:], psum[:, b:b + 2, D], 1.0 / DH, None, ALU.mult).then_inc(hm, 1)
                    dve.tensor_scalar(degm[:], psum[:, b:b + 2, D + 4], DEG_EPS, None,
                                      ALU.max).then_inc(deg_max, 1)
                    dve.wait_ge(hm, upto(p))
                    dve.tensor_tensor(h_mean2[:], h_mean[:], h_mean[:], ALU.mult).then_inc(hm2, 1)
                    dve.wait_ge(deg_max, upto(p))
                    dve.reciprocal(rdeg[(k - 1) % 2][:], degm[:]).then_inc(deg_inv, 1)
                    dve.wait_ge(hm2, upto(p))
                    dve.scalar_tensor_tensor(out=h_var[:], in0=psum[:, b:b + 2, D + 2], scalar=1.0 / DH,
                                             in1=h_mean2[:], op0=ALU.mult, op1=ALU.subtract).then_inc(hv, 1)
                    dve.wait_ge(hv, upto(p))
                    dve.tensor_scalar(h_veps[:], h_var[:], 0.0, LN_EPS, ALU.max, ALU.add).then_inc(hve, 1)
                    dve.wait_ge(hstd, upto(p))
                    dve.reciprocal(h_rstd[:], h_std[:]).then_inc(hrstd, 1)
                    dve.wait_ge(hrstd, upto(p))
                    if begun(p - 1):
                        dve.wait_ge(p_lo, upto(p - 1))
                    for g in range(2):
                        last = dve.scalar_tensor_tensor(out=p_f[:, g, :], in0=psum[:, b + g, 0:D],
                                                        scalar=h_rstd[:, g:g + 1], in1=betaW[:],
                                                        op0=ALU.mult, op1=ALU.add)
                    last.then_inc(p_made, 1)
                if active("Tr", n):
                    dve.wait_ge(gt_hi, upto(n))
                    split_lo(GT[k % 2], psum[:, bank("Tr", k), 0:2 * C].rearrange("p (g c) -> p g c", g=2), gt_lo)
                if active("AXB", n):
                    p = n - 2
                    b = bank("AXB", k)
                    dve.wait_ge(pe_did["AXB"], upto(p))
                    dve.wait_ge(xa_out, upto(p))
                    dve.wait_ge(deg_inv, upto(p))
                    for g in range(2):
                        last = dve.scalar_tensor_tensor(out=agg[:, g, :], in0=psum[:, b, g * D:(g + 1) * D],
                                                        scalar=rdeg[(k - 2) % 2][:, g:g + 1],
                                                        in1=xa[:, g, :], op0=ALU.mult, op1=ALU.add)
                    last.then_inc(agg_made, 1)
                    dve.wait_ge(agg_made, upto(p))
                    dve.scalar_tensor_tensor(out=n2.s[:], in0=agg[:], scalar=0.0, in1=x1[:],
                                             op0=ALU.max, op1=ALU.add).then_inc(n2.summed, 1)
                    stats(n2, p)
                if active("H1W", n):
                    if begun(n - 3):
                        dve.wait_ge(h1w_hi, upto(n - 3))
                    split_lo(h1w, flat(bank("H1W", k)), h1w_lo)
                if active("AXB", n):
                    p = n - 2
                    if begun(p - 1):
                        dve.wait_ge(x2_lo, upto(p - 1))
                    if begun(p - 1):
                        dve.wait_ge(x2_hi, upto(p - 1))
                    if begun(p - 1):
                        dve.wait_ge(x2c_made, upto(p - 1))
                    apply(n2, p, x2)
                if active("AP3", n):
                    p = n - 4
                    dve.wait_ge(n3.done, upto(p))
                    if begun(p - 1):
                        dve.wait_ge(tk_relu, upto(p - 1))
                    for g in range(2):
                        last = dve.tensor_scalar(nz[:, g, :], x3[:, g, :], 0.0, 0.0, ALU.not_equal, ALU.add,
                                                 accum_out=nz_count[:, g:g + 1])
                    last.then_inc(x3_nz, 1)
                    dve.wait_ge(x3_nz, upto(p))
                    dve.tensor_scalar(mask[:], nz_count[:], 0.0, None, ALU.is_gt).then_inc(mask_made, 1)
                if active("Ax3", n):
                    if begun(n - 4):
                        dve.wait_ge(ax3_hi, upto(n - 4))
                    split_lo(ax3, flat(bank("Ax3", k)), ax3_lo)
                if active("Gx", n):
                    dve.wait_ge(gx_hi, upto(n))
                    split_lo(gx, flat(bank("Gx", k)), gx_lo)
                if active("GP", n):
                    p = n - 1
                    dve.wait_ge(pe_did["GP"], upto(p))
                    dve.wait_ge(xb_made, upto(p))
                    dve.scalar_tensor_tensor(out=n1.s[:].rearrange("p g d -> p (g d)"),
                                             in0=xb[:].rearrange("p g d -> p (g d)"), scalar=2.0,
                                             in1=flat(bank("GP", k)), op0=ALU.mult,
                                             op1=ALU.add).then_inc(n1.summed, 1)
                    stats(n1, p)
                if active("H2", n):
                    p = n - 3
                    dve.wait_ge(h2_relu, upto(p))
                    if begun(p - 1):
                        dve.wait_ge(pe_did["H2W"], upto(p - 1))
                    dve.tensor_copy(h2_s[0][:], h2_f[:]).then_inc(h2_hi, 1)
                if active("GP", n):
                    p = n - 1
                    if begun(p - 1):
                        dve.wait_ge(pe_did["xT"], upto(p - 1))
                    apply(n1, p, x1)

            steps(dve, body)

        @block.gpsimd
        def _(pool):
            def lo(dst, src, signal):
                return pool.tensor_tensor(dst[1][:], src, f(dst[0][:]), ALU.subtract).then_inc(signal, 1)

            pool.wait_ge(w_ready, 1)

            def body(n, k):
                if active("prep", n):
                    pool.wait_ge(be_lo, upto(n))
                    if begun(n - 1):
                        pool.wait_ge(pe_did["G"], upto(n - 1))
                    for h in range(2):
                        last = pool.tensor_tensor(BH[:, h], f(HT[:]), bc(be_parts[:, h, :], [C, 2, C], 2), ALU.mult)
                    last.then_inc(bh_made, 1)
                if active("R", n):
                    p = n - 1
                    pool.wait_ge(r_hi[0], upto(p))
                    if begun(p - 1):
                        pool.wait_ge(pe_did["P"], upto(p - 1))
                    pool.tensor_tensor(r_s[1][:, 0:2], r_f[:, 0:2], f(r_s[0][:, 0:2]), ALU.subtract)
                    pool.wait_ge(r_hi[1], upto(p))
                    pool.tensor_tensor(r_s[1][:, 2:4], r_f[:, 2:4], f(r_s[0][:, 2:4]),
                                       ALU.subtract).then_inc(r_lo, 1)
                    pool.wait_ge(sq_made, upto(p))
                    pool.tensor_tensor(sq2[:], sq[:, 0:2], sq[:, 2:4], ALU.add).then_inc(sq_half, 1)
                    pool.wait_ge(sq_half, upto(p))
                    pool.tensor_tensor(sq1[:], sq2[:, 0], sq2[:, 1], ALU.add).then_inc(sq_sum, 1)
                    pool.wait_ge(a_hi, upto(p))
                    lo(A[(k - 1) % RING], at_in[:, (k - 1) % RING], a_lo)
                if active("H1", n):
                    if begun(n - 3):
                        pool.wait_ge(h1_hi, upto(n - 3))
                    lo(h1_s, h1_f[:], h1_lo)
                if active("AP3", n):
                    if begun(n - 4):
                        pool.wait_ge(x3_hi, upto(n - 4))
                    lo(x3s, x3[:], x3_lo)
                if active("prep", n):
                    pool.wait_ge(xs_hi, upto(n))
                    lo(xs, x_in[:, k % RING], xs_lo)
                if active("P", n):
                    if begun(n - 1):
                        pool.wait_ge(p_hi, upto(n - 1))
                    lo(p_s, p_f[:], p_lo)
                if active("GP", n):
                    p = n - 1
                    if begun(p - 1):
                        pool.wait_ge(n1.summed, upto(p - 1))
                    pool.tensor_tensor(xb[:], x_in[:, (k - 1) % RING], bc(b2half[:], [C, 2, D], 1),
                                       ALU.add).then_inc(xb_made, 1)
                if active("AXB", n):
                    p = n - 2
                    pool.wait_ge(x2_hi, upto(p))
                    lo(x2s, x2[:], x2_lo)
                    if begun(p - 2):
                        pool.wait_ge(n3.summed, upto(p - 2))
                    pool.tensor_tensor(x2c[(k - 2) % 2][:], x2[:], bc(c3_b[:], [C, 2, D], 1),
                                       ALU.add).then_inc(x2c_made, 1)
                if active("H2", n):
                    if begun(n - 3):
                        pool.wait_ge(h2_hi, upto(n - 3))
                    lo(h2_s, h2_f[:], h2_lo)

            steps(pool, body)


def kernel(x, adj, L0_gnn_W1, L0_gnn_b1, L0_gnn_gamma, L0_gnn_beta, L0_gnn_W2, L0_gnn_b2, L1_gnn_W,
           L2_gnn_W1, L2_gnn_b1, L2_gnn_W2, L2_gnn_b2, L2_gnn_W3, L2_gnn_b3, L3_gnn_kernel):
    import numpy as np
    import concourse.bacc as bacc
    from concourse.bass_utils import run_bass_kernel_spmd

    x, adj = np.asarray(x), np.asarray(adj)
    N, C, D = x.shape

    def chunks(w):
        w = np.asarray(w)
        return np.ascontiguousarray(w.reshape(w.shape[0] // C, C, w.shape[1]).transpose(1, 0, 2))

    def column(v):
        return np.ascontiguousarray(np.asarray(v).reshape(-1, C).T)

    arrays = {
        "x_in_dram": np.ascontiguousarray(x.reshape(N // 2, 2, C, D).transpose(0, 2, 1, 3)),
        "adjT": np.ascontiguousarray(adj.reshape(N // 2, 2, C, C).transpose(0, 3, 1, 2)),
        "w1T_in": chunks(np.asarray(L0_gnn_W1).T), "w2T_in": chunks(np.asarray(L0_gnn_W2).T),
        "gamma": column(L0_gnn_gamma), "beta": column(L0_gnn_beta), "b1": column(L0_gnn_b1),
        "b2": np.asarray(L0_gnn_b2), "wT": np.ascontiguousarray(np.asarray(L1_gnn_W).T),
        "v1": chunks(L2_gnn_W1), "v2": chunks(L2_gnn_W2), "v3": chunks(L2_gnn_W3),
        "c1": column(L2_gnn_b1), "c2": column(L2_gnn_b2), "c3": np.asarray(L2_gnn_b3),
        "wk": chunks(L3_gnn_kernel), "eye": np.eye(C, dtype=np.float32),
    }
    nc = bacc.Bacc("TRN2", target_bir_lowering=False, num_devices=1)
    args = [nc.dram_tensor(name, a.shape, mybir.dt.from_np(a.dtype), kind="ExternalInput").ap()
            for name, a in arrays.items()]
    order = ["x_in_dram", "adjT", "w1T_in", "w2T_in", "gamma", "beta", "b1", "b2", "wT", "v1", "v2", "v3",
             "c1", "c2", "c3", "wk", "eye"]
    by_name = dict(zip(arrays, args))
    out = nc.dram_tensor("out", (N // 2, C, 2, D), F32, kind="ExternalOutput").ap()
    build(nc, *[by_name[o] for o in order], out)
    r = run_bass_kernel_spmd(nc, [arrays], core_ids=[0])
    got = r.results[0]["out"]
    return np.ascontiguousarray(got.transpose(0, 2, 1, 3)).reshape(N, C, D)
```

```python
from contextlib import ExitStack

import concourse.bass as bass
from concourse import mybir

F32 = mybir.dt.float32
F32R = mybir.dt.float32r
ALU = mybir.AluOpType
ACT = mybir.ActivationFunctionType
AX_X = mybir.AxisListType.X

LN_EPS = 1e-5
DEG_EPS = 1e-6
TINY = 1.1754944e-38

LAG = dict(prep=-1, G=0, Tr=0, Gx=0,
           R=1, P=1, GP=1,
           x1=2, xT=2, XAB=2, AXB=2,
           x2=3, Ax2=3, H1=3, H1W=3, H2=3,
           H2W=4, AP3=4, Ax3=4, TK=4,
           F=5)
BANK = dict(R=0, Ax2=0, Tr=0, GP=0, H1=1, Gx=1, XAB=2, AXB=2, TK=2, H2=3, xT=4, P=4,
            H2W=6, H1W=6, G=7, AP3=7, Ax3=7)
BANKS = 8
UNROLL = 4
FIRST_IN_LOOP = 8


def build(nc, x, adjT, w1T, w2T, gamma, beta, b1, b2, wT, v1, v2, v3, c1, c2, c3, wk, eye, out):
    NP, C, GP_, D = x.shape
    DH = w1T.shape[2]
    KD, KH = D // C, DH // C
    assert (C, GP_, D, DH) == (128, 2, 256, 512) and NP % UNROLL == 0 and NP > FIRST_IN_LOOP
    END = NP + LAG["F"]

    with ExitStack() as ctx:
        def sb(name, shape, dt=F32):
            return ctx.enter_context(nc.sbuf_tensor(name, [C, *shape], dt))

        def hi_lo(name, shape):
            return [sb(f"{name}_hi", shape, F32R), sb(f"{name}_lo", shape, F32R)]

        def sem(name):
            return ctx.enter_context(nc.semaphore(name))

        psum = ctx.enter_context(nc.psum_tensor("psum", [C, BANKS, 512], F32))

        w2g = sb("w2g", [KH, D])
        w1T_s, w2c_s = hi_lo("w1T", [KD, DH]), hi_lo("w2c", [KH, D + 2])
        wab_s, wk_s = hi_lo("wab", [KD, 2 * D]), hi_lo("wk", [KD, D])
        v_s = [hi_lo(f"v{j}", [KD, D]) for j in range(3)]
        gamma_c, beta_c, b1_c = sb("gamma_c", [KH]), sb("beta_c", [KH]), sb("b1_c", [KH])
        c1_c, c2_c = sb("c1_c", [KD]), sb("c2_c", [KD])
        b2_b, b2half, c3_b = sb("b2_b", [D]), sb("b2half", [D]), sb("c3_b", [D])
        beta_b, w2mean, betaW = sb("beta_b", [KH, C]), sb("w2mean", [D]), sb("betaW", [D])
        ones, ident = sb("ones", [C]), sb("ident", [C])
        ones_r = sb("ones_r", [2], F32R)
        eps_c, wait_pad = sb("eps_c", [1]), sb("wait_pad", [1])

        RING = 4
        x_in = sb("x_in", [RING, 2, D])
        at_in = sb("at_in", [RING, 2, C])
        HT = sb("HT", [2, C], F32R)
        ht_count, be = sb("ht_count", [2]), sb("be", [2])
        be_r, be_parts = sb("be_r", [2], F32R), sb("be_parts", [2, 2])
        BH = sb("BH", [2, 2, C + 2], F32R)
        dn_max, dn_inv, dinv = sb("dn_max", [2]), sb("dn_inv", [2]), sb("dinv", [2])
        Gd = sb("Gd", [2, C])
        GT = [sb(f"GT{b}", [2, C]) for b in range(2)]
        gx = hi_lo("gx", [KD, 2, C])
        r_f, r_s = sb("r_f", [KH, 2, C]), hi_lo("r", [KH, 2, C])
        sq, sq2, sq1 = sb("sq", [KH, 2, C]), sb("sq2", [2, 2, C]), sb("sq1", [2, C])
        h_mean2, h_var = sb("h_mean2", [2]), sb("h_var", [2])
        h_veps, h_std, h_rstd = sb("h_veps", [2]), sb("h_std", [2]), sb("h_rstd", [2])
        p_f = sb("p_f", [2, D])
        xb = sb("xb", [2, D])
        A = [hi_lo(f"A{b}", [2, C]) for b in range(RING)]
        A_f = [sb(f"A{b}_f", [2, C]) for b in range(RING)]
        degm, rdeg = sb("degm", [2]), sb("rdeg", [2])
        x1 = sb("x1", [2, D])
        x1T = hi_lo("x1T", [KD, 2, C])
        xa, xbw, agg = sb("xa", [2, D]), hi_lo("xbw", [2, D + 2]), sb("agg", [2, D])
        x2, x2c = sb("x2", [2, D]), [sb(f"x2c{b}", [2, D]) for b in range(2)]
        ax2 = hi_lo("ax2", [KD, 2, C])
        h1_f, h1_s, h1w = sb("h1_f", [KD, 2, C]), hi_lo("h1", [KD, 2, C]), sb("h1w", [2, D])
        h2_f, h2_s, h2w = sb("h2_f", [KD, 2, C]), hi_lo("h2", [KD, 2, C]), hi_lo("h2w", [2, D])
        x3 = sb("x3", [2, D])
        nz, nz_count, mask = sb("nz", [2, D]), sb("nz_count", [2]), sb("mask", [2])
        ax3 = hi_lo("ax3", [KD, 2, C])
        tk = sb("tk", [2, D])
        x4 = [sb(f"x4{b}", [2, D]) for b in range(2)]
        w1T_f = r_f[:].rearrange("p (k a) g c -> p k (a g c)", k=KD)
        w2T_f = sq[:].rearrange("p m g c -> p m (g c)")
        wab_f = [h1_f[:].rearrange("p m g c -> p (m g c)"), h2_f[:].rearrange("p m g c -> p (m g c)")]
        v_f, wk_f = [xa[:], agg[:], x2[:]], tk[:]
        class Norm:
            def __init__(self, name):
                self.s = sb(f"{name}_s", [2, D])
                self.st, self.mv = sb(f"{name}_st", [2, 6]), sb(f"{name}_mv", [2, 2])
                self.std, self.rstd = sb(f"{name}_std", [2]), sb(f"{name}_rstd", [2])
                self.shift, self.shifted = sb(f"{name}_shift", [2]), sem(f"{name}_shifted")
                self.summed, self.stats = sem(f"{name}_summed"), sem(f"{name}_stats")
                self.varied, self.rooted = sem(f"{name}_varied"), sem(f"{name}_rooted")
                self.inverted, self.done = sem(f"{name}_inverted"), sem(f"{name}_done")
        n1, n2, n3, n4 = Norm("n1"), Norm("n2"), Norm("n3"), Norm("n4")

        load_w, w_prep_step, w_prep, w_ps, w_ready = (
            sem(s) for s in ("load_w", "w_prep_step", "w_prep", "w_ps", "w_ready"))
        x_loaded, at_loaded = ([sem(f"{name}_loaded{j}") for j in range(RING)] for name in ("x", "at"))
        stored = [sem(f"stored{j}") for j in range(2)]
        pe_did = {s: sem(f"pe_{s}") for s in BANK}
        pe_R0 = sem("pe_R0")
        ht_made, ht_counted, be_max, be_made, be_hi, be_lo, bh_made = (
            sem(s) for s in ("ht_made", "ht_counted", "be_max", "be_made", "be_hi", "be_lo", "bh_made"))
        dn_1, dn_2, dn_3, gd_made = sem("dn_1"), sem("dn_2"), sem("dn_3"), sem("gd_made")
        w_hi, w_lo, gt_made, gx_hi, gx_lo = (sem(s) for s in ("w_hi", "w_lo", "gt_made", "gx_hi", "gx_lo"))
        r_relu, r_hi = [sem(f"r_relu{j}") for j in range(2)], [sem(f"r_hi{j}") for j in range(2)]
        r_lo, sq_made, sq_half, sq_sum = sem("r_lo"), sem("sq_made"), sem("sq_half"), sem("sq_sum")
        hm2, hv, hve, hstd, hrstd = (sem(s) for s in ("h_mean2", "h_var", "h_veps", "h_std", "h_rstd"))
        deg_max, deg_inv = sem("deg_max"), sem("deg_inv")
        p_made, xb_made = sem("p_made"), sem("xb_made")
        a_hi, a_lo, a_copied = sem("a_hi"), sem("a_lo"), sem("a_copied")
        x1T_hi, x1T_lo = sem("x1T_hi"), sem("x1T_lo")
        xa_out, xbw_hi, xbw_lo = sem("xa_out"), sem("xbw_hi"), sem("xbw_lo")
        agg_made = sem("agg_made")
        x2c_made = sem("x2c_made")
        ax2_hi, ax2_lo = sem("ax2_hi"), sem("ax2_lo")
        h1_relu, h1_hi, h1_lo, h1w_out = (sem(s) for s in ("h1_relu", "h1_hi", "h1_lo", "h1w_out"))
        h2_relu, h2_hi, h2_lo, h2w_hi, h2w_lo = (sem(s) for s in ("h2_relu", "h2_hi", "h2_lo", "h2w_hi", "h2w_lo"))
        x3_nz, mask_made = sem("x3_nz"), sem("mask_made")
        tk_masked = sem("tk_masked")
        ax3_hi, ax3_lo, tk_relu = sem("ax3_hi"), sem("ax3_lo"), sem("tk_relu")

        def begun(pair):
            return not isinstance(pair, int) or pair >= 0

        def upto(pair):
            return min(pair, NP - 1) + 1 if isinstance(pair, int) else pair + 1

        def active(stage, n):
            return not isinstance(n, int) or 0 <= n - LAG[stage] < NP

        def steps(eng, body):
            stop = NP - UNROLL
            for n in range(LAG["prep"], FIRST_IN_LOOP):
                body(n, n)
            with eng.Fori(FIRST_IN_LOOP, stop - UNROLL + 1, UNROLL) as base:
                for k in range(UNROLL):
                    body(base + k, k)
            for n in range(stop, END):
                body(n, n)

        def at_count(p, k):
            if isinstance(p, int):
                return 16 * (p // RING + 1)
            return (p + (RING - k % RING)) * (16 // RING)

        def f(ap):
            return ap.bitcast(F32)

        def bc(ap, shape, axis):
            return ap.unsqueeze(axis).to_broadcast(shape)

        block = ctx.enter_context(nc.Block())

        @block.sync
        def _(sp):
            wTk = wT.rearrange("(h k p) d -> h p k d", h=2, p=C)
            for dst, src in (
                (w1T_f, w1T), (w2T_f, w2T), (gamma_c[:], gamma), (beta_c[:], beta), (b1_c[:], b1),
                *((wab_f[kk][:, h * D:(h + 1) * D], wTk[h, :, kk]) for h in range(2) for kk in range(KD)),
                (v_f[0], v1), (v_f[1], v2), (v_f[2], v3), (wk_f, wk),
                (c1_c[:], c1), (c2_c[:], c2), (ident[:], eye),
                (b2_b[:], b2.partition_broadcast(C)), (c3_b[:], c3.partition_broadcast(C)),
            ):
                sp.dma_start(dst, src).then_inc(load_w, 16)

            def load(pair, k):
                sp.dma_start(at_in[:, k % RING], adjT[pair]).then_inc(at_loaded[k % RING], 16)
                sp.dma_start(x_in[:, k % RING], x[pair]).then_inc(x_loaded[k % RING], 16)

            load(0, 0)

            def body(n, k):
                if not isinstance(n, int) or n + 2 < NP:
                    if begun(n - 2):
                        sp.wait_ge(pe_did["Gx"], upto(n - 2))
                    if begun(n - 2):
                        sp.wait_ge(xb_made, upto(n - 2))
                    if begun(n - 2):
                        sp.wait_ge(pe_did["G"], upto(n - 2))
                    if begun(n - 2):
                        sp.wait_ge(w_lo, upto(n - 2))
                        sp.wait_ge(a_copied, upto(n - 2))
                        sp.wait_ge(a_lo, upto(n - 2))
                    if isinstance(n, int):
                        load(n + 2, k + 2)
                    else:
                        sp.dma_start(at_in[:, (k + 2) % RING],
                                     adjT[bass.ds(n + 2, 1)].rearrange("a p g c -> p (a g) c")
                                     ).then_inc(at_loaded[(k + 2) % RING], 16)
                        sp.dma_start(x_in[:, (k + 2) % RING],
                                     x[bass.ds(n + 2, 1)].rearrange("a p g c -> p (a g) c")
                                     ).then_inc(x_loaded[(k + 2) % RING], 16)
                if active("F", n):
                    p = n - LAG["F"]
                    sp.wait_ge(n4.done, upto(p))
                    src = x4[(k - LAG["F"]) % 2]
                    if isinstance(p, int):
                        sp.dma_start(out[p], src[:]).then_inc(stored[(k - 5) % 2], 16)
                    else:
                        sp.dma_start(out[bass.ds(p, 1)].rearrange("a p g c -> p (a g) c"),
                                     src[:]).then_inc(stored[(k - 5) % 2], 16)

            steps(sp, body)
            for j in range(2):
                sp.wait_ge(stored[j], 16 * NP // 2)

        @block.tensor
        def _(pe):
            def mm(o, a, b, start, stop):
                return pe.matmul(o, a, b, start=start, stop=stop)

            def product(o, terms):
                last = None
                for t, (a, b) in enumerate(terms):
                    last = mm(o, a[0], b[0], t == 0, False)
                    mm(o, a[0], b[1], False, False)
                    last = mm(o, a[1], b[0], False, t == len(terms) - 1)
                return last

            def part(s, *idx):
                return [s[0][idx], s[1][idx]]

            ALL = slice(None)

            def cols(m):
                return slice(m * C, (m + 1) * C)

            pe.wait_ge(load_w, 16 * 18)
            pe.wait_ge(w_prep, 1)
            for m in range(KH):
                mm(psum[:, 0, 0:D], ones[:], w2g[:, m, :], m == 0, m == KH - 1)
            for m in range(KH):
                last = mm(psum[:, 1, 0:D], beta_b[:, m, :], w2T_f[:, m, :], m == 0, m == KH - 1)
            last.then_inc(w_ps, 1)
            pe.wait_ge(w_ready, 1)

            def propagate_T(stage, state, adj):
                for m in range(KD):
                    for g in range(2):
                        last = mm(psum[:, BANK[stage], (2 * m + g) * C:(2 * m + g + 1) * C],
                                  state[:, g, cols(m)], adj[:, g, :], True, True)
                last.then_inc(pe_did[stage], 1)

            def weigh(stage, stateT, w):
                for g in range(2):
                    last = product(psum[:, BANK[stage], g * D:(g + 1) * D],
                                   [(part(stateT, ALL, m, g), part(w, ALL, m)) for m in range(KD)])
                last.then_inc(pe_did[stage], 1)

            def body(n, k):
                if active("R", n):
                    p = n - 1
                    pe.wait_ge(gx_hi, upto(p))
                    pe.wait_ge(gx_lo, upto(p))
                    for m in range(KH):
                        if m == 2 and begun(n - 2):
                            pe.wait_ge(n1.summed, upto(n - 2))
                        o = psum[:, BANK["R"] + 1 - m // 2, (m % 2) * 2 * C:(m % 2 + 1) * 2 * C]
                        last = product(o, [(part(w1T_s, ALL, kk, cols(m)), part(gx, ALL, kk))
                                           for kk in range(KD)])
                        if m == 1:
                            last.then_inc(pe_R0, 1)
                    last.then_inc(pe_did["R"], 1)
                if active("G", n):
                    p = n
                    pe.wait_ge(bh_made, upto(p))
                    pe.wait_ge(w_lo, upto(p))
                    if begun(n - 5):
                        pe.wait_ge(ax3_lo, upto(n - 5))
                    for g in range(2):
                        o = psum[:, BANK["G"], g * (C + 2):(g + 1) * (C + 2)]
                        mm(o, HT[:, g, :], BH[:, 0, g, :], True, False)
                        last = mm(o, HT[:, g, :], BH[:, 1, g, :], False, True)
                    last.then_inc(pe_did["G"], 1)
                if active("xT", n):
                    p = n - 2
                    pe.wait_ge(n1.done, upto(p))
                    pe.wait_ge(p_made, upto(p))
                    for m in range(KD):
                        for g in range(2):
                            last = pe.transpose(psum[:, BANK["xT"], (2 * m + g) * C:(2 * m + g + 1) * C],
                                                x1[:, g, cols(m)], ident[:])
                    last.then_inc(pe_did["xT"], 1)
                if active("H2W", n):
                    p = n - 4
                    pe.wait_ge(h2_hi, upto(p))
                    pe.wait_ge(h2_lo, upto(p))
                    pe.wait_ge(h1w_out, upto(p))
                    weigh("H2W", h2_s, v_s[2])
                if active("Ax2", n):
                    p = n - 3
                    pe.wait_ge(n2.done, upto(p))
                    pe.wait_ge(a_copied, upto(p))
                    pe.wait_ge(r_relu[1], upto(n - 1))
                    propagate_T("Ax2", x2, A_f[(k - 3) % RING])
                if active("XAB", n):
                    p = n - 2
                    pe.wait_ge(x1T_hi, upto(p))
                    pe.wait_ge(x1T_lo, upto(p))
                    if begun(n - 4):
                        pe.wait_ge(h2_relu, upto(n - 4))
                    if begun(n - 5):
                        pe.wait_ge(tk_relu, upto(n - 5))
                    for g in range(2):
                        last = product(psum[:, BANK["XAB"] + g, :],
                                       [(part(x1T, ALL, m, g), part(wab_s, ALL, m)) for m in range(KD)])
                    last.then_inc(pe_did["XAB"], 1)
                if active("H1", n):
                    p = n - 3
                    pe.wait_ge(ax2_hi, upto(p))
                    pe.wait_ge(ax2_lo, upto(p))
                    pe.wait_ge(r_relu[0], upto(n - 1))
                    for m in range(KD):
                        last = product(psum[:, BANK["H1"], m * 2 * C:(m + 1) * 2 * C],
                                       [(part(v_s[0], ALL, kk, cols(m)), part(ax2, ALL, kk)) for kk in range(KD)])
                    last.then_inc(pe_did["H1"], 1)
                if active("AP3", n):
                    p = n - 4
                    pe.wait_ge(h2w_hi, upto(p))
                    pe.wait_ge(h2w_lo, upto(p))
                    pe.wait_ge(gd_made, upto(n))
                    for g in range(2):
                        last = product(psum[:, BANK["AP3"], g * D:(g + 1) * D],
                                       [(part(A[(k - 4) % RING], ALL, g), part(h2w, ALL, g))])
                    last.then_inc(pe_did["AP3"], 1)
                if active("P", n):
                    p = n - 1
                    pe.wait_ge(r_hi[1], upto(p))
                    pe.wait_ge(r_lo, upto(p))
                    pe.wait_ge(sq_sum, upto(p))
                    if begun(n - 2):
                        pe.wait_ge(x1T_lo, upto(n - 2))
                        pe.wait_ge(p_made, upto(n - 2))
                    for g in range(2):
                        product(psum[:, BANK["P"] + g, 0:D + 2],
                                [(part(r_s, ALL, m, g), part(w2c_s, ALL, m)) for m in range(KH)])
                        last = mm(psum[:, BANK["P"] + g, D + 2:D + 3], sq1[:, g, :], ones[:, 0:1], True, True)
                    last.then_inc(pe_did["P"], 1)
                if active("Tr", n):
                    p = n
                    pe.wait_ge(gd_made, upto(p))
                    if begun(n - 3):
                        pe.wait_ge(ax2_lo, upto(n - 3))
                    for g in range(2):
                        last = pe.transpose(psum[:, BANK["Tr"], cols(g)], Gd[:, g, :], ident[:])
                    last.then_inc(pe_did["Tr"], 1)
                if active("AXB", n):
                    p = n - 2
                    pe.wait_ge(xbw_hi, upto(p))
                    pe.wait_ge(xbw_lo, upto(p))
                    pe.wait_ge(a_hi, upto(p))
                    pe.wait_ge(a_lo, upto(p))
                    for g in range(2):
                        last = product(psum[:, BANK["AXB"] + g, 0:D + 2],
                                       [(part(A[(k - 2) % RING], ALL, g), part(xbw, ALL, g))])
                    last.then_inc(pe_did["AXB"], 1)
                if active("H1W", n):
                    p = n - 3
                    pe.wait_ge(h1_hi, upto(p))
                    pe.wait_ge(h1_lo, upto(p))
                    if begun(n - 4):
                        pe.wait_ge(h2w_lo, upto(n - 4))
                    weigh("H1W", h1_s, v_s[1])
                if active("Ax3", n):
                    p = n - 4
                    pe.wait_ge(n3.done, upto(p))
                    propagate_T("Ax3", x3, A_f[(k - 4) % RING])
                if active("Gx", n):
                    p = n
                    pe.wait_ge(gt_made, upto(p))
                    pe.wait_ge(x_loaded[k % RING], at_count(p, k))
                    if begun(n - 3):
                        pe.wait_ge(h1_relu, upto(n - 3))
                    propagate_T("Gx", x_in[:, k % RING], GT[k % 2])
                if active("GP", n):
                    p = n - 1
                    pe.wait_ge(p_made, upto(p))
                    pe.wait_ge(gt_made, upto(n))
                    for g in range(2):
                        last = mm(psum[:, BANK["GP"], g * D:(g + 1) * D], GT[(k - 1) % 2][:, g, :],
                                  p_f[:, g, :], True, True)
                    last.then_inc(pe_did["GP"], 1)
                if active("H2", n):
                    p = n - 3
                    pe.wait_ge(h1w_out, upto(p))
                    if begun(n - 2):
                        pe.wait_ge(agg_made, upto(n - 2))
                    propagate_T("H2", h1w, A_f[(k - 3) % RING])
                if active("TK", n):
                    p = n - 4
                    pe.wait_ge(ax3_hi, upto(p))
                    pe.wait_ge(ax3_lo, upto(p))
                    pe.wait_ge(agg_made, upto(n - 2))
                    weigh("TK", ax3, wk_s)

            steps(pe, body)

        @block.scalar
        def _(act):
            def copy(o, i):
                return act.activation(o, i, ACT.Copy)

            def split_hi(stage, dst, signal, p, used):
                act.wait_ge(pe_did[stage], upto(p))
                if begun(p - 1):
                    act.wait_ge(used, upto(p - 1))
                copy(dst[0][:].rearrange("p a b -> p (a b)") if len(dst[0].shape) == 3 else
                     dst[0][:].rearrange("p a b c -> p (a b c)"),
                     psum[:, BANK[stage], 0:2 * D]).then_inc(signal, 1)

            def root(nm, p):
                act.wait_ge(nm.varied, upto(p))
                if begun(p - 1):
                    act.wait_ge(nm.inverted, upto(p - 1))
                act.activation(nm.std[:], nm.mv[:, :, 1], ACT.Sqrt, bias=eps_c[:, 0:1]).then_inc(nm.rooted, 1)

            act.wait_ge(w_ready, 1)

            def relu_out(stage, m, dst, bias, extra=0):
                return act.activation(dst[:, m].rearrange("p g c -> p (g c)"),
                                      psum[:, BANK[stage] + extra, (m % 2) * 2 * C:(m % 2 + 1) * 2 * C],
                                      ACT.Relu, bias=bias[:, m:m + 1])

            def body(n, k):
                if active("x2", n):
                    p = n - 3
                    act.wait_ge(n2.shifted, upto(p))
                    if begun(p - 1):
                        act.wait_ge(pe_did["Ax2"], upto(p - 1))
                        act.wait_ge(x2c_made, upto(p - 1))
                    for g in range(2):
                        last = act.activation(x2[:, g, :], n2.s[:, g, :], ACT.Identity,
                                              scale=n2.rstd[:, g:g + 1], bias=n2.shift[:, g:g + 1])
                    last.then_inc(n2.done, 1)
                if active("R", n):
                    p = n - 1
                    act.wait_ge(pe_R0, upto(p))
                    if begun(p - 1):
                        act.wait_ge(sq_made, upto(p - 1))
                        act.wait_ge(r_lo, upto(p - 1))
                    relu_out("R", 0, r_f, b1_c, 1)
                    relu_out("R", 1, r_f, b1_c, 1).then_inc(r_relu[0], 1)
                    act.wait_ge(pe_did["R"], upto(p))
                    relu_out("R", 2, r_f, b1_c)
                    relu_out("R", 3, r_f, b1_c).then_inc(r_relu[1], 1)
                if active("xT", n):
                    split_hi("xT", x1T, x1T_hi, n - 2, pe_did["XAB"])
                if active("R", n):
                    p = n - 1
                    act.wait_ge(r_relu[0], upto(p))
                    if begun(p - 1):
                        act.wait_ge(pe_did["P"], upto(p - 1))
                    copy(r_s[0][:, 0:2], r_f[:, 0:2]).then_inc(r_hi[0], 1)
                if active("H2W", n):
                    split_hi("H2W", h2w, h2w_hi, n - 4, pe_did["AP3"])
                if active("R", n):
                    act.wait_ge(r_relu[1], upto(n - 1))
                    copy(r_s[0][:, 2:4], r_f[:, 2:4]).then_inc(r_hi[1], 1)
                if active("Ax2", n):
                    split_hi("Ax2", ax2, ax2_hi, n - 3, pe_did["H1"])
                if active("R", n):
                    p = n - 1
                    if begun(p - 1):
                        act.wait_ge(sq_half, upto(p - 1))
                    act.activation(sq[:], r_f[:], ACT.Square).then_inc(sq_made, 1)
                    act.wait_ge(at_loaded[(k - 1) % RING], at_count(p, k - 1))
                    if begun(n - 5):
                        act.wait_ge(pe_did["Ax3"], upto(n - 5))
                    copy(A[(k - 1) % RING][0][:], at_in[:, (k - 1) % RING]).then_inc(a_hi, 1)
                    copy(A_f[(k - 1) % RING][:], at_in[:, (k - 1) % RING]).then_inc(a_copied, 1)
                if active("XAB", n):
                    p = n - 2
                    act.wait_ge(pe_did["XAB"], upto(p))
                    if begun(p - 1):
                        act.wait_ge(pe_did["AXB"], upto(p - 1))
                    b = BANK["XAB"]
                    copy(xbw[0][:, :, 0:D], psum[:, b:b + 2, D:2 * D]).then_inc(xbw_hi, 1)
                    if begun(p - 1):
                        act.wait_ge(agg_made, upto(p - 1))
                    copy(xa[:], psum[:, b:b + 2, 0:D]).then_inc(xa_out, 1)
                if active("H1", n):
                    p = n - 3
                    act.wait_ge(pe_did["H1"], upto(p))
                    if begun(p - 1):
                        act.wait_ge(h1_lo, upto(p - 1))
                    relu_out("H1", 0, h1_f, c1_c)
                    relu_out("H1", 1, h1_f, c1_c).then_inc(h1_relu, 1)
                    act.wait_ge(h1_relu, upto(p))
                    if begun(p - 1):
                        act.wait_ge(pe_did["H1W"], upto(p - 1))
                    copy(h1_s[0][:], h1_f[:]).then_inc(h1_hi, 1)
                if active("AP3", n):
                    root(n3, n - 4)
                if active("F", n):
                    root(n4, n - 5)
                if active("P", n):
                    b = BANK["P"]
                    act.wait_ge(pe_did["P"], upto(n - 1))
                    act.activation(h_mean2[:], psum[:, b:b + 2, D], ACT.Square, scale=1.0 / DH).then_inc(hm2, 1)
                if active("Tr", n):
                    p = n
                    act.wait_ge(pe_did["Tr"], upto(p))
                    if begun(p - 2):
                        act.wait_ge(pe_did["GP"], upto(p - 2))
                    copy(GT[k % 2][:].rearrange("p a b -> p (a b)"),
                         psum[:, BANK["Tr"], 0:2 * C]).then_inc(gt_made, 1)
                if active("P", n):
                    act.wait_ge(hve, upto(n - 1))
                    act.activation(h_std[:], h_veps[:], ACT.Sqrt).then_inc(hstd, 1)
                if active("H1W", n):
                    p = n - 3
                    act.wait_ge(pe_did["H1W"], upto(p))
                    if begun(p - 1):
                        act.wait_ge(pe_did["H2"], upto(p - 1))
                    copy(h1w[:].rearrange("p g d -> p (g d)"),
                         psum[:, BANK["H1W"], 0:2 * D]).then_inc(h1w_out, 1)
                if active("Ax3", n):
                    split_hi("Ax3", ax3, ax3_hi, n - 4, pe_did["TK"])
                if active("Gx", n):
                    split_hi("Gx", gx, gx_hi, n, pe_did["R"])
                if active("F", n):
                    p = n - 5
                    act.wait_ge(n4.shifted, upto(p))
                    if not isinstance(p, int):
                        act.wait_ge(stored[(k - 5) % 2], (p - (k - 5) % 2) * 8)
                    elif p >= 2:
                        act.wait_ge(stored[p % 2], 16 * (p // 2))
                    for g in range(2):
                        last = act.activation(x4[(k - 5) % 2][:, g, :], n4.s[:, g, :], ACT.Identity,
                                              scale=n4.rstd[:, g:g + 1], bias=n4.shift[:, g:g + 1])
                    last.then_inc(n4.done, 1)
                if active("H2", n):
                    p = n - 3
                    act.wait_ge(pe_did["H2"], upto(p))
                    if begun(p - 1):
                        act.wait_ge(h2_lo, upto(p - 1))
                    relu_out("H2", 0, h2_f, c2_c)
                    relu_out("H2", 1, h2_f, c2_c).then_inc(h2_relu, 1)
                if active("H2", n):
                    p = n - 3
                    act.wait_ge(h2_relu, upto(p))
                    if begun(p - 1):
                        act.wait_ge(pe_did["H2W"], upto(p - 1))
                    copy(h2_s[0][:], h2_f[:]).then_inc(h2_hi, 1)
                if active("AXB", n):
                    root(n2, n - 2)
                if active("TK", n):
                    p = n - 4
                    act.wait_ge(pe_did["TK"], upto(p))
                    if begun(p - 1):
                        act.wait_ge(tk_masked, upto(p - 1))
                    act.activation(tk[:].rearrange("p g d -> p (g d)"), psum[:, BANK["TK"], 0:2 * D],
                                   ACT.Relu).then_inc(tk_relu, 1)
                if active("GP", n):
                    root(n1, n - 1)

            steps(act, body)

        @block.vector
        def _(dve):
            def split_lo(dst, src, signal):
                return dve.tensor_tensor(dst[1][:], src, f(dst[0][:]), ALU.subtract).then_inc(signal, 1)

            chain = [0]

            def setup(ins):
                chain[0] += 1
                ins.then_inc(w_prep_step, 1)
                dve.wait_ge(w_prep_step, chain[0])

            dve.wait_ge(load_w, 16 * 18)
            dve.memset(ones[:], 1.0)
            dve.memset(eps_c[:], LN_EPS)
            setup(dve.tensor_scalar(b2half[:], b2_b[:], 0.5, None, ALU.mult))
            for m in range(KH):
                setup(dve.tensor_scalar(w2g[:, m, :], w2T_f[:, m, :], gamma_c[:, m:m + 1], None, ALU.mult))
                setup(dve.tensor_scalar(beta_b[:, m, :], ones[:], beta_c[:, m:m + 1], None, ALU.mult))
            setup(dve.tensor_copy(ones_r[:], ones[:, 0:2]))
            dve.nop().then_inc(w_prep, 1)
            for (hi, lo), src in (
                ([s[:] for s in w1T_s], w1T_f), ([s[:, 0] for s in wab_s], wab_f[0]),
                ([s[:, 1] for s in wab_s], wab_f[1]), ([s[:] for s in wk_s], wk_f),
                *(([s[:] for s in v_s[j]], v_f[j]) for j in range(3)),
            ):
                setup(dve.tensor_copy(hi, src))
                setup(dve.tensor_tensor(lo, src, f(hi), ALU.subtract))
            dve.wait_ge(w_ps, 1)
            setup(dve.tensor_scalar(w2mean[:], psum[:, 0, 0:D], 1.0 / DH, None, ALU.mult))
            setup(dve.tensor_copy(betaW[:], psum[:, 1, 0:D]))
            setup(dve.tensor_tensor(w2T_f, w2g[:], bc(w2mean[:], [C, KH, D], 1), ALU.subtract))
            hi, lo = w2c_s
            setup(dve.tensor_copy(hi[:, :, 0:D], w2T_f))
            setup(dve.tensor_tensor(lo[:, :, 0:D], w2T_f, f(hi[:, :, 0:D]), ALU.subtract))
            setup(dve.tensor_copy(hi[:, :, D:D + 1], ones[:, 0:KH].unsqueeze(2)))
            setup(dve.tensor_scalar(hi[:, :, D + 1:D + 2], ones[:, 0:KH].unsqueeze(2), 0.0, None, ALU.mult))
            setup(dve.tensor_scalar(lo[:, :, D:D + 2], ones[:, 0:2 * KH].rearrange("p (a b) -> p a b", a=KH),
                                    0.0, None, ALU.mult))
            pair01 = ones[:, 0:2].unsqueeze(2)
            setup(dve.tensor_copy(xbw[0][:, :, D:D + 1], pair01))
            setup(dve.tensor_scalar(xbw[0][:, :, D + 1:D + 2], pair01, 0.0, None, ALU.mult))
            for h in range(2):
                setup(dve.tensor_scalar(xbw[1][:, :, D + h:D + h + 1], pair01, 0.0, None, ALU.mult))
                setup(dve.tensor_scalar(BH[:, h, :, C + 1:C + 2], pair01, 0.0, None, ALU.mult))
            dve.nop().then_inc(w_ready, 1)

            def stats(nm, p):
                dve.wait_ge(nm.summed, upto(p))
                for g in range(2):
                    last = dve.bn_stats(nm.st[:, g, :], nm.s[:, g, :])
                last.then_inc(nm.stats, 1)

            def mean_var(nm):
                for g in range(2):
                    last = dve.bn_aggr(nm.mv[:, g, :], nm.st[:, g, :])
                last.then_inc(nm.varied, 1)

            def invert(nm, p):
                dve.wait_ge(nm.rooted, upto(p))
                if begun(p - 1):
                    dve.wait_ge(nm.done, upto(p - 1))
                dve.reciprocal(nm.rstd[:], nm.std[:]).then_inc(nm.inverted, 1)

            def shift(nm, p):
                dve.wait_ge(nm.inverted, upto(p))
                dve.scalar_tensor_tensor(out=nm.shift[:], in0=nm.mv[:, :, 0], scalar=-1.0, in1=nm.rstd[:],
                                         op0=ALU.mult, op1=ALU.mult).then_inc(nm.shifted, 1)

            def apply(nm, p, dst):
                dve.wait_ge(nm.inverted, upto(p))
                for g in range(2):
                    last = dve.tensor_scalar(dst[:, g, :], nm.s[:, g, :], nm.mv[:, g, 0:1], nm.rstd[:, g:g + 1],
                                             ALU.subtract, ALU.mult)
                last.then_inc(nm.done, 1)

            def flat(b):
                return psum[:, b, 0:2 * D]

            def body(n, k):
                if active("x1", n):
                    invert(n1, n - 2)
                if active("x1", n):
                    p = n - 2
                    if begun(p - 1):
                        dve.wait_ge(pe_did["xT"], upto(p - 1))
                    apply(n1, p, x1)
                if active("F", n):
                    p = n - 5
                    dve.wait_ge(n3.done, upto(p))
                    if begun(p - 1):
                        dve.wait_ge(n4.summed, upto(p - 1))
                    for g in range(2):
                        last = dve.tensor_scalar(nz[:, g, :], x3[:, g, :], 0.0, 0.0, ALU.not_equal, ALU.add,
                                                 accum_out=nz_count[:, g:g + 1])
                    last.then_inc(x3_nz, 1)
                    dve.wait_ge(x3_nz, upto(p))
                    dve.tensor_scalar(mask[:], nz_count[:], 0.0, None, ALU.is_gt).then_inc(mask_made, 1)
                if active("xT", n):
                    dve.wait_ge(x1T_hi, upto(n - 2))
                    split_lo(x1T, flat(BANK["xT"]), x1T_lo)
                if active("H2W", n):
                    dve.wait_ge(h2w_hi, upto(n - 4))
                    split_lo(h2w, flat(BANK["H2W"]), h2w_lo)
                if active("Ax2", n):
                    dve.wait_ge(ax2_hi, upto(n - 3))
                    split_lo(ax2, flat(BANK["Ax2"]), ax2_lo)

                q = n + 1
                g_dn = psum[:, BANK["G"], 0:2 * (C + 2)].rearrange("p (g c) -> p g c", g=2)
                dn = g_dn[:, :, C]
                w = at_in[:, (k + 1) % RING, :, 0:1]
                if active("G", n):
                    dve.wait_ge(pe_did["G"], upto(n))
                    dve.tensor_scalar(dn_max[:], dn, TINY, None, ALU.max).then_inc(dn_1, 1)
                if active("prep", n):
                    dve.wait_ge(at_loaded[(k + 1) % RING], at_count(q, k + 1))
                    if begun(n):
                        dve.wait_ge(pe_did["G"], upto(n))
                    dve.tensor_scalar(HT[:], at_in[:, (k + 1) % RING], 0.0, None,
                                      ALU.not_equal).then_inc(ht_made, 1)
                if active("G", n):
                    dve.wait_ge(dn_1, upto(n))
                    dve.reciprocal(dn_inv[:], dn_max[:]).then_inc(dn_2, 1)
                if active("prep", n):
                    dve.wait_ge(ht_made, upto(q))
                    dve.tensor_reduce(ht_count[:], f(HT[:]), AX_X, ALU.add).then_inc(ht_counted, 1)
                if active("G", n):
                    dve.wait_ge(dn_2, upto(n))
                    dve.scalar_tensor_tensor(out=dinv[:], in0=dn, scalar=0.0, in1=dn_inv[:],
                                             op0=ALU.is_gt, op1=ALU.mult).then_inc(dn_3, 1)
                if active("prep", n):
                    dve.tensor_copy(BH[:, 0, :, C:C + 1], w).then_inc(w_hi, 1)
                    dve.wait_ge(ht_counted, upto(q))
                    dve.tensor_scalar(be[:], ht_count[:], 1.0, None, ALU.max).then_inc(be_max, 1)
                if active("G", n):
                    dve.wait_ge(dn_3, upto(n))
                    if begun(n - 1):
                        dve.wait_ge(pe_did["Tr"], upto(n - 1))
                    dve.tensor_tensor(Gd[:], g_dn[:, :, 0:C], bc(dinv[:], [C, 2, C], 2),
                                      ALU.mult).then_inc(gd_made, 1)
                if active("prep", n):
                    dve.wait_ge(be_max, upto(q))
                    if begun(q - 1):
                        dve.wait_ge(bh_made, upto(q - 1))
                    dve.reciprocal(be_parts[:, 1, :], be[:]).then_inc(be_made, 1)
                    dve.wait_ge(w_hi, upto(q))
                    dve.tensor_tensor(BH[:, 1, :, C:C + 1], w, f(BH[:, 0, :, C:C + 1]),
                                      ALU.subtract).then_inc(w_lo, 1)
                    dve.wait_ge(be_made, upto(q))
                    dve.tensor_copy(be_r[:], be_parts[:, 1, :]).then_inc(be_hi, 1)
                if active("prep", n):
                    dve.wait_ge(be_hi, upto(q))
                    dve.tensor_copy(be_parts[:, 0, :], f(be_r[:]))
                    dve.tensor_tensor(be_parts[:, 1, :], be_parts[:, 1, :], f(be_r[:]),
                                      ALU.subtract).then_inc(be_lo, 1)

                if active("AP3", n):
                    p = n - 4
                    dve.wait_ge(pe_did["AP3"], upto(p))
                    dve.wait_ge(x2c_made, upto(p))
                    dve.tensor_tensor(n3.s[:].rearrange("p g d -> p (g d)"), flat(BANK["AP3"]),
                                      x2c[(k - 4) % 2][:].rearrange("p g d -> p (g d)"),
                                      ALU.add).then_inc(n3.summed, 1)
                    stats(n3, p)
                if active("XAB", n):
                    p = n - 2
                    dve.wait_ge(xbw_hi, upto(p))
                    dve.wait_ge(xa_out, upto(p))
                    if active("AP3", n):
                        dve.wait_ge(n3.stats, upto(n - 4))
                    dve.tensor_tensor(xbw[1][:, :, 0:D], psum[:, BANK["XAB"]:BANK["XAB"] + 2, D:2 * D],
                                      f(xbw[0][:, :, 0:D]), ALU.subtract).then_inc(xbw_lo, 1)
                elif active("AP3", n):
                    dve.wait_ge(n3.stats, upto(n - 4))
                    dve.memset(wait_pad[:], 0.0)
                if active("AP3", n):
                    mean_var(n3)
                if active("F", n):
                    stats(n4, n - 5)
                if active("AP3", n):
                    p = n - 4
                    invert(n3, p)
                if active("F", n):
                    dve.wait_ge(n4.stats, upto(n - 5))
                    dve.memset(wait_pad[:], 0.0)
                    mean_var(n4)
                b = BANK["P"]
                if active("AP3", n):
                    p = n - 4
                    if begun(p - 1):
                        dve.wait_ge(pe_did["Ax3"], upto(p - 1))
                        dve.wait_ge(n4.summed, upto(p - 1))
                    apply(n3, p, x3)
                if active("P", n):
                    dve.wait_ge(hm2, upto(n - 1))
                    dve.scalar_tensor_tensor(out=h_var[:], in0=psum[:, b:b + 2, D + 2], scalar=1.0 / DH,
                                             in1=h_mean2[:], op0=ALU.mult, op1=ALU.subtract).then_inc(hv, 1)
                if active("P", n):
                    dve.wait_ge(hv, upto(n - 1))
                    dve.tensor_scalar(h_veps[:], h_var[:], 0.0, LN_EPS, ALU.max, ALU.add).then_inc(hve, 1)
                if active("AXB", n):
                    dve.wait_ge(pe_did["AXB"], upto(n - 2))
                    dve.tensor_scalar(degm[:], psum[:, BANK["AXB"]:BANK["AXB"] + 2, D], DEG_EPS, None,
                                      ALU.max).then_inc(deg_max, 1)
                if active("F", n):
                    invert(n4, n - 5)
                if active("P", n):
                    dve.wait_ge(hstd, upto(n - 1))
                    dve.reciprocal(h_rstd[:], h_std[:]).then_inc(hrstd, 1)
                if active("AXB", n):
                    dve.wait_ge(deg_max, upto(n - 2))
                    dve.reciprocal(rdeg[:], degm[:]).then_inc(deg_inv, 1)
                if active("F", n):
                    shift(n4, n - 5)
                if active("P", n):
                    p = n - 1
                    dve.wait_ge(hrstd, upto(p))
                    if begun(p - 1):
                        dve.wait_ge(pe_did["GP"], upto(p - 1))
                    for g in range(2):
                        last = dve.scalar_tensor_tensor(out=p_f[:, g, :], in0=psum[:, b + g, 0:D],
                                                        scalar=h_rstd[:, g:g + 1], in1=betaW[:],
                                                        op0=ALU.mult, op1=ALU.add)
                    last.then_inc(p_made, 1)

                if active("AXB", n):
                    p = n - 2
                    dve.wait_ge(xa_out, upto(p))
                    dve.wait_ge(deg_inv, upto(p))
                    for g in range(2):
                        last = dve.scalar_tensor_tensor(out=agg[:, g, :], in0=psum[:, BANK["AXB"] + g, 0:D],
                                                        scalar=rdeg[:, g:g + 1],
                                                        in1=xa[:, g, :], op0=ALU.mult, op1=ALU.add)
                    last.then_inc(agg_made, 1)
                if active("Ax3", n):
                    dve.wait_ge(ax3_hi, upto(n - 4))
                    split_lo(ax3, flat(BANK["Ax3"]), ax3_lo)
                if active("AXB", n):
                    p = n - 2
                    dve.wait_ge(agg_made, upto(p))
                    if begun(p - 1):
                        dve.wait_ge(n2.done, upto(p - 1))
                    dve.scalar_tensor_tensor(out=n2.s[:], in0=agg[:], scalar=0.0, in1=x1[:],
                                             op0=ALU.max, op1=ALU.add).then_inc(n2.summed, 1)
                if active("Gx", n):
                    dve.wait_ge(gx_hi, upto(n))
                    split_lo(gx, flat(BANK["Gx"]), gx_lo)
                if active("AXB", n):
                    stats(n2, n - 2)
                    dve.wait_ge(n2.stats, upto(n - 2))
                    dve.memset(wait_pad[:], 0.0)
                    mean_var(n2)
                if active("GP", n):
                    p = n - 1
                    dve.wait_ge(pe_did["GP"], upto(p))
                    dve.wait_ge(xb_made, upto(p))
                    dve.scalar_tensor_tensor(out=n1.s[:].rearrange("p g d -> p (g d)"),
                                             in0=xb[:].rearrange("p g d -> p (g d)"), scalar=2.0,
                                             in1=flat(BANK["GP"]), op0=ALU.mult,
                                             op1=ALU.add).then_inc(n1.summed, 1)
                    stats(n1, p)
                if active("AXB", n):
                    if active("GP", n):
                        dve.wait_ge(n1.stats, upto(n - 1))
                    invert(n2, n - 2)
                elif active("GP", n):
                    dve.wait_ge(n1.stats, upto(n - 1))
                    dve.memset(wait_pad[:], 0.0)
                if active("GP", n):
                    mean_var(n1)
                if active("AXB", n):
                    shift(n2, n - 2)

            steps(dve, body)

        @block.gpsimd
        def _(pool):
            def lo(dst, src, signal):
                return pool.tensor_tensor(dst[1][:], src, f(dst[0][:]), ALU.subtract).then_inc(signal, 1)

            pool.wait_ge(w_ready, 1)

            def body(n, k):
                if active("F", n):
                    p = n - 5
                    pool.wait_ge(tk_relu, upto(p))
                    pool.wait_ge(mask_made, upto(p))
                    if begun(p - 1):
                        pool.wait_ge(n4.done, upto(p - 1))
                    pool.tensor_tensor(n4.s[:], tk[:], bc(mask[:], [C, 2, D], 2), ALU.mult).then_inc(tk_masked, 1)
                if active("R", n):
                    p = n - 1
                    pool.wait_ge(r_hi[0], upto(p))
                    if begun(p - 1):
                        pool.wait_ge(pe_did["P"], upto(p - 1))
                    pool.tensor_tensor(r_s[1][:, 0:2], r_f[:, 0:2], f(r_s[0][:, 0:2]), ALU.subtract)
                    pool.wait_ge(r_hi[1], upto(p))
                    pool.tensor_tensor(r_s[1][:, 2:4], r_f[:, 2:4], f(r_s[0][:, 2:4]),
                                       ALU.subtract).then_inc(r_lo, 1)
                    pool.wait_ge(sq_made, upto(p))
                    pool.tensor_tensor(sq2[:], sq[:, 0:2], sq[:, 2:4], ALU.add).then_inc(sq_half, 1)
                    pool.wait_ge(sq_half, upto(p))
                    pool.tensor_tensor(sq1[:], sq2[:, 0], sq2[:, 1], ALU.add).then_inc(sq_sum, 1)
                    pool.wait_ge(a_hi, upto(p))
                    lo(A[(k - 1) % RING], at_in[:, (k - 1) % RING], a_lo)
                if active("F", n):
                    pool.wait_ge(tk_masked, upto(n - 5))
                    pool.tensor_tensor(n4.s[:], n4.s[:], x3[:], ALU.add).then_inc(n4.summed, 1)
                if active("H1", n):
                    pool.wait_ge(h1_hi, upto(n - 3))
                    lo(h1_s, h1_f[:], h1_lo)
                if active("prep", n):
                    q = n + 1
                    pool.wait_ge(be_lo, upto(q))
                    if begun(n):
                        pool.wait_ge(pe_did["G"], upto(n))
                    for h in range(2):
                        last = pool.tensor_tensor(BH[:, h, :, 0:C], f(HT[:]), bc(be_parts[:, h, :], [C, 2, C], 2),
                                                  ALU.mult)
                    last.then_inc(bh_made, 1)
                if active("x2", n):
                    p = n - 3
                    pool.wait_ge(n2.done, upto(p))
                    if begun(p - 2):
                        pool.wait_ge(n3.summed, upto(p - 2))
                    pool.tensor_tensor(x2c[(k - 3) % 2][:], x2[:], bc(c3_b[:], [C, 2, D], 1),
                                       ALU.add).then_inc(x2c_made, 1)
                if active("GP", n):
                    p = n - 1
                    if begun(p - 1):
                        pool.wait_ge(n1.summed, upto(p - 1))
                    pool.tensor_tensor(xb[:], x_in[:, (k - 1) % RING], bc(b2half[:], [C, 2, D], 1),
                                       ALU.add).then_inc(xb_made, 1)
                if active("H2", n):
                    pool.wait_ge(h2_hi, upto(n - 3))
                    lo(h2_s, h2_f[:], h2_lo)

            steps(pool, body)


def kernel(x, adj, L0_gnn_W1, L0_gnn_b1, L0_gnn_gamma, L0_gnn_beta, L0_gnn_W2, L0_gnn_b2, L1_gnn_W,
           L2_gnn_W1, L2_gnn_b1, L2_gnn_W2, L2_gnn_b2, L2_gnn_W3, L2_gnn_b3, L3_gnn_kernel):
    import numpy as np
    import concourse.bacc as bacc
    from concourse.bass_utils import run_bass_kernel_spmd

    x, adj = np.asarray(x), np.asarray(adj)
    N, C, D = x.shape

    def chunks(w):
        w = np.asarray(w)
        return np.ascontiguousarray(w.reshape(w.shape[0] // C, C, w.shape[1]).transpose(1, 0, 2))

    def column(v):
        return np.ascontiguousarray(np.asarray(v).reshape(-1, C).T)

    arrays = {
        "x_in_dram": np.ascontiguousarray(x.reshape(N // 2, 2, C, D).transpose(0, 2, 1, 3)),
        "adjT": np.ascontiguousarray(adj.reshape(N // 2, 2, C, C).transpose(0, 3, 1, 2)),
        "w1T_in": chunks(np.asarray(L0_gnn_W1).T), "w2T_in": chunks(np.asarray(L0_gnn_W2).T),
        "gamma": column(L0_gnn_gamma), "beta": column(L0_gnn_beta), "b1": column(L0_gnn_b1),
        "b2": np.asarray(L0_gnn_b2), "wT": np.ascontiguousarray(np.asarray(L1_gnn_W).T),
        "v1": chunks(L2_gnn_W1), "v2": chunks(L2_gnn_W2), "v3": chunks(L2_gnn_W3),
        "c1": column(L2_gnn_b1), "c2": column(L2_gnn_b2), "c3": np.asarray(L2_gnn_b3),
        "wk": chunks(L3_gnn_kernel), "eye": np.eye(C, dtype=np.float32),
    }
    nc = bacc.Bacc("TRN2", target_bir_lowering=False, num_devices=1)
    args = [nc.dram_tensor(name, a.shape, mybir.dt.from_np(a.dtype), kind="ExternalInput").ap()
            for name, a in arrays.items()]
    order = ["x_in_dram", "adjT", "w1T_in", "w2T_in", "gamma", "beta", "b1", "b2", "wT", "v1", "v2", "v3",
             "c1", "c2", "c3", "wk", "eye"]
    by_name = dict(zip(arrays, args))
    out = nc.dram_tensor("out", (N // 2, C, 2, D), F32, kind="ExternalOutput").ap()
    build(nc, *[by_name[o] for o in order], out)
    r = run_bass_kernel_spmd(nc, [arrays], core_ids=[0])
    got = r.results[0]["out"]
    return np.ascontiguousarray(got.transpose(0, 2, 1, 3)).reshape(N, C, D)
```

```python
from contextlib import ExitStack

import concourse.bass as bass
from concourse import mybir

F32 = mybir.dt.float32
F32R = mybir.dt.float32r
ALU = mybir.AluOpType
ACT = mybir.ActivationFunctionType
AX_X = mybir.AxisListType.X

LN_EPS = 1e-5
DEG_EPS = 1e-6
TINY = 1.1754944e-38

LAG = dict(prep=-1, G=0, Tr=0, Gx=0,
           R=1, P=1, GP=1,
           x1=2, xT=2, XAB=2, AXB=2,
           x2=3, Ax2=3, H1=3, H1W=3, H2=3,
           H2W=4, AP3=4, Ax3=4, TK=4,
           F=5)
BANK = dict(R=0, Ax2=0, Tr=0, GP=0, H1=1, Gx=1, XAB=2, AXB=2, TK=2, H2=3, xT=4, P=4,
            H2W=6, H1W=6, G=7, AP3=7, Ax3=7)
BANKS = 8
UNROLL = 4
FIRST_IN_LOOP = 8


def build(nc, x, adjT, w1T, w2T, wab, v1, v2, v3, wk, columns, rows, eye, out):
    NP, C, GP_, D = x.shape
    DH = w1T.shape[2]
    KD, KH = D // C, DH // C
    assert (C, GP_, D, DH) == (128, 2, 256, 512) and NP % UNROLL == 0 and NP > FIRST_IN_LOOP
    END = NP + LAG["F"]

    with ExitStack() as ctx:
        def sb(name, shape, dt=F32):
            return ctx.enter_context(nc.sbuf_tensor(name, [C, *shape], dt))

        def hi_lo(name, shape):
            return [sb(f"{name}_hi", shape, F32R), sb(f"{name}_lo", shape, F32R)]

        def sem(name):
            return ctx.enter_context(nc.semaphore(name))

        psum = ctx.enter_context(nc.psum_tensor("psum", [C, BANKS, 512], F32))

        w2g = sb("w2g", [KH, D])
        w1T_s, w2c_s = hi_lo("w1T", [KD, DH]), hi_lo("w2c", [KH, D + 2])
        wab_s, wk_s = hi_lo("wab", [KD, 2 * D]), hi_lo("wk", [KD, D])
        v_s = [hi_lo(f"v{j}", [KD, D]) for j in range(3)]
        columns_s, rows_b = sb("columns", [3 * KH + 2 * KD]), sb("rows", [2, D])
        gamma_c, beta_c, b1_c = (columns_s[:, j * KH:(j + 1) * KH] for j in range(3))
        c1_c, c2_c = (columns_s[:, 3 * KH + j * KD:3 * KH + (j + 1) * KD] for j in range(2))
        b2half, c3_b = sb("b2half", [D]), rows_b[:, 1]
        beta_b, w2mean, betaW = sb("beta_b", [KH, C]), sb("w2mean", [D]), sb("betaW", [D])
        ones, ident = sb("ones", [C]), sb("ident", [C])
        eps_c, wait_pad = sb("eps_c", [1]), sb("wait_pad", [1])

        RING = 4
        x_in = sb("x_in", [RING, 2, D])
        at_in = sb("at_in", [RING, 2, C])
        HT = sb("HT", [2, C], F32R)
        ht_count, be = sb("ht_count", [2]), sb("be", [2])
        be_r, be_parts = sb("be_r", [2], F32R), sb("be_parts", [2, 2])
        BH = sb("BH", [2, 2, C + 2], F32R)
        dn_max, dn_inv, dinv = sb("dn_max", [2]), sb("dn_inv", [2]), sb("dinv", [2])
        Gd = sb("Gd", [2, C])
        GT = [sb(f"GT{b}", [2, C]) for b in range(2)]
        gx = hi_lo("gx", [KD, 2, C])
        r_f, r_s = sb("r_f", [KH, 2, C]), hi_lo("r", [KH, 2, C])
        sq, sq2, sq1 = sb("sq", [KH, 2, C]), sb("sq2", [2, 2, C]), sb("sq1", [2, C])
        h_mean2, h_var = sb("h_mean2", [2]), sb("h_var", [2])
        h_veps, h_std, h_rstd = sb("h_veps", [2]), sb("h_std", [2]), sb("h_rstd", [2])
        p_f = sb("p_f", [2, D])
        xb = sb("xb", [2, D])
        A = [hi_lo(f"A{b}", [2, C]) for b in range(RING)]
        A_f = [sb(f"A{b}_f", [2, C]) for b in range(RING)]
        degm, rdeg = sb("degm", [2]), sb("rdeg", [2])
        x1 = sb("x1", [2, D])
        x1T = hi_lo("x1T", [KD, 2, C])
        xa, xbw, agg = sb("xa", [2, D]), hi_lo("xbw", [2, D + 2]), sb("agg", [2, D])
        x2, x2c = sb("x2", [2, D]), [sb(f"x2c{b}", [2, D]) for b in range(2)]
        ax2 = hi_lo("ax2", [KD, 2, C])
        h1_f, h1_s, h1w = sb("h1_f", [KD, 2, C]), hi_lo("h1", [KD, 2, C]), sb("h1w", [2, D])
        h2_f, h2_s, h2w = sb("h2_f", [KD, 2, C]), hi_lo("h2", [KD, 2, C]), hi_lo("h2w", [2, D])
        x3 = sb("x3", [2, D])
        nz, nz_count, mask = sb("nz", [2, D]), sb("nz_count", [2]), sb("mask", [2])
        ax3 = hi_lo("ax3", [KD, 2, C])
        tk = sb("tk", [2, D])
        x4 = [sb(f"x4{b}", [2, D]) for b in range(2)]
        w1T_f = r_f[:].rearrange("p (k a) g c -> p k (a g c)", k=KD)
        wab_f = [h1_f[:].rearrange("p m g c -> p (m g c)"), h2_f[:].rearrange("p m g c -> p (m g c)")]
        v_f, wk_f = [xa[:], agg[:], x2[:]], tk[:]
        class Norm:
            def __init__(self, name):
                self.s = sb(f"{name}_s", [2, D])
                self.st, self.mv = sb(f"{name}_st", [2, 6]), sb(f"{name}_mv", [2, 2])
                self.std, self.rstd = sb(f"{name}_std", [2]), sb(f"{name}_rstd", [2])
                self.shift, self.shifted = sb(f"{name}_shift", [2]), sem(f"{name}_shifted")
                self.summed, self.stats = sem(f"{name}_summed"), sem(f"{name}_stats")
                self.varied, self.rooted = sem(f"{name}_varied"), sem(f"{name}_rooted")
                self.inverted, self.done = sem(f"{name}_inverted"), sem(f"{name}_done")
        n1, n2, n3, n4 = Norm("n1"), Norm("n2"), Norm("n3"), Norm("n4")
        w2T_f = [n3.s[:], n4.s[:]]

        small_loaded, w1_loaded, w2_loaded, wab_loaded, v_loaded = (
            sem(s) for s in ("small_loaded", "w1_loaded", "w2_loaded", "wab_loaded", "v_loaded"))
        table_loaded = sem("table_loaded")
        consts_step, consts_made, w1_hi, w1_lo, w2_scaled, w2_sums, w2_mean, w2_centred, w2c_hi, w2c_lo = (
            sem(s) for s in ("consts_step", "consts_made", "w1_hi", "w1_lo", "w2_scaled", "w2_sums", "w2_mean",
                             "w2_centred", "w2c_hi", "w2c_lo"))
        betaW_sums, betaW_made, wab_hi, wab_lo, v_hi, v_lo = (
            sem(s) for s in ("betaW_sums", "betaW_made", "wab_hi", "wab_lo", "v_hi", "v_lo"))
        x_loaded, at_loaded = ([sem(f"{name}_loaded{j}") for j in range(RING)] for name in ("x", "at"))
        stored = [sem(f"stored{j}") for j in range(2)]
        pe_did = {s: sem(f"pe_{s}") for s in BANK}
        pe_R0 = sem("pe_R0")
        ht_made, ht_counted, be_max, be_made, be_hi, be_lo, bh_made = (
            sem(s) for s in ("ht_made", "ht_counted", "be_max", "be_made", "be_hi", "be_lo", "bh_made"))
        dn_1, dn_2, dn_3, gd_made = sem("dn_1"), sem("dn_2"), sem("dn_3"), sem("gd_made")
        w_hi, w_lo, gt_made, gx_hi, gx_lo = (sem(s) for s in ("w_hi", "w_lo", "gt_made", "gx_hi", "gx_lo"))
        r_relu, r_hi = [sem(f"r_relu{j}") for j in range(2)], [sem(f"r_hi{j}") for j in range(2)]
        r_lo, sq_made, sq_half, sq_sum = sem("r_lo"), sem("sq_made"), sem("sq_half"), sem("sq_sum")
        hm2, hv, hve, hstd, hrstd = (sem(s) for s in ("h_mean2", "h_var", "h_veps", "h_std", "h_rstd"))
        deg_max, deg_inv = sem("deg_max"), sem("deg_inv")
        p_made, xb_made = sem("p_made"), sem("xb_made")
        a_hi, a_lo, a_copied = sem("a_hi"), sem("a_lo"), sem("a_copied")
        x1T_hi, x1T_lo = sem("x1T_hi"), sem("x1T_lo")
        xa_out, xbw_hi, xbw_lo = sem("xa_out"), sem("xbw_hi"), sem("xbw_lo")
        agg_made = sem("agg_made")
        x2c_made = sem("x2c_made")
        ax2_hi, ax2_lo = sem("ax2_hi"), sem("ax2_lo")
        h1_relu, h1_hi, h1_lo, h1w_out = (sem(s) for s in ("h1_relu", "h1_hi", "h1_lo", "h1w_out"))
        h2_relu, h2_hi, h2_lo, h2w_hi, h2w_lo = (sem(s) for s in ("h2_relu", "h2_hi", "h2_lo", "h2w_hi", "h2w_lo"))
        x3_nz, mask_made = sem("x3_nz"), sem("mask_made")
        tk_masked = sem("tk_masked")
        ax3_hi, ax3_lo, tk_relu = sem("ax3_hi"), sem("ax3_lo"), sem("tk_relu")

        def begun(pair):
            return not isinstance(pair, int) or pair >= 0

        def upto(pair):
            return min(pair, NP - 1) + 1 if isinstance(pair, int) else pair + 1

        def first(n, j):
            return isinstance(n, int) and n == j

        def active(stage, n):
            return not isinstance(n, int) or 0 <= n - LAG[stage] < NP

        def steps(eng, body):
            stop = NP - UNROLL
            for n in range(LAG["prep"], FIRST_IN_LOOP):
                body(n, n)
            with eng.Fori(FIRST_IN_LOOP, stop - UNROLL + 1, UNROLL) as base:
                for k in range(UNROLL):
                    body(base + k, k)
            for n in range(stop, END):
                body(n, n)

        def at_count(p, k):
            if isinstance(p, int):
                return 16 * (p // RING + 1)
            return (p + (RING - k % RING)) * (16 // RING)

        def f(ap):
            return ap.bitcast(F32)

        def bc(ap, shape, axis):
            return ap.unsqueeze(axis).to_broadcast(shape)

        block = ctx.enter_context(nc.Block())

        @block.sync
        def _(sp):
            def load(pair, k):
                sp.dma_start(at_in[:, k % RING], adjT[pair]).then_inc(at_loaded[k % RING], 16)
                sp.dma_start(x_in[:, k % RING], x[pair]).then_inc(x_loaded[k % RING], 16)

            load(0, 0)
            sp.dma_start(ident[:], eye).then_inc(small_loaded, 16)
            sp.dma_start(columns_s[:], columns).then_inc(small_loaded, 16)
            sp.dma_start(rows_b[:], rows.partition_broadcast(C)).then_inc(small_loaded, 16)
            sp.dma_start(w1T_f, w1T).then_inc(w1_loaded, 16)
            for h in range(2):
                sp.dma_start(w2T_f[h], w2T[:, 2 * h:2 * h + 2]).then_inc(w2_loaded, 16)

            def body(n, k):
                if first(n, 0):
                    for kk in range(KD):
                        sp.dma_start(wab_f[kk], wab[:, kk]).then_inc(wab_loaded, 16)
                    for dst, src in ((v_f[0], v1), (v_f[1], v2), (v_f[2], v3), (wk_f, wk)):
                        sp.dma_start(dst, src).then_inc(v_loaded, 16)
                if not isinstance(n, int) or n + 2 < NP:
                    if begun(n - 2):
                        sp.wait_ge(pe_did["Gx"], upto(n - 2))
                        sp.wait_ge(xb_made, upto(n - 2))
                        sp.wait_ge(pe_did["G"], upto(n - 2))
                        sp.wait_ge(w_lo, upto(n - 2))
                        sp.wait_ge(a_copied, upto(n - 2))
                        sp.wait_ge(a_lo, upto(n - 2))
                    if isinstance(n, int):
                        load(n + 2, k + 2)
                    else:
                        sp.dma_start(at_in[:, (k + 2) % RING],
                                     adjT[bass.ds(n + 2, 1)].rearrange("a p g c -> p (a g) c")
                                     ).then_inc(at_loaded[(k + 2) % RING], 16)
                        sp.dma_start(x_in[:, (k + 2) % RING],
                                     x[bass.ds(n + 2, 1)].rearrange("a p g c -> p (a g) c")
                                     ).then_inc(x_loaded[(k + 2) % RING], 16)
                if active("F", n):
                    p = n - LAG["F"]
                    sp.wait_ge(n4.done, upto(p))
                    src = x4[(k - LAG["F"]) % 2]
                    if isinstance(p, int):
                        sp.dma_start(out[p], src[:]).then_inc(stored[(k - 5) % 2], 16)
                    else:
                        sp.dma_start(out[bass.ds(p, 1)].rearrange("a p g c -> p (a g) c"),
                                     src[:]).then_inc(stored[(k - 5) % 2], 16)

            steps(sp, body)
            for j in range(2):
                sp.wait_ge(stored[j], 16 * NP // 2)

        @block.tensor
        def _(pe):
            def mm(o, a, b, start, stop):
                return pe.matmul(o, a, b, start=start, stop=stop)

            def product(o, terms):
                for t, (a, b) in enumerate(terms):
                    mm(o, a[0], b[0], t == 0, False)
                    mm(o, a[0], b[1], False, False)
                    last = mm(o, a[1], b[0], False, t == len(terms) - 1)
                return last

            def part(s, *idx):
                return [s[0][idx], s[1][idx]]

            ALL = slice(None)

            def cols(m):
                return slice(m * C, (m + 1) * C)

            def propagate_T(stage, state, adj):
                for m in range(KD):
                    for g in range(2):
                        last = mm(psum[:, BANK[stage], (2 * m + g) * C:(2 * m + g + 1) * C],
                                  state[:, g, cols(m)], adj[:, g, :], True, True)
                last.then_inc(pe_did[stage], 1)

            def weigh(stage, stateT, w):
                for g in range(2):
                    last = product(psum[:, BANK[stage], g * D:(g + 1) * D],
                                   [(part(stateT, ALL, m, g), part(w, ALL, m)) for m in range(KD)])
                last.then_inc(pe_did[stage], 1)

            def body(n, k):
                if active("R", n):
                    p = n - 1
                    pe.wait_ge(gx_hi, upto(p))
                    pe.wait_ge(gx_lo, upto(p))
                    if first(n, 1):
                        pe.wait_ge(w1_lo, 1)
                    for m in range(KH):
                        if m == 2 and begun(n - 2):
                            pe.wait_ge(n1.summed, upto(n - 2))
                        o = psum[:, BANK["R"] + 1 - m // 2, (m % 2) * 2 * C:(m % 2 + 1) * 2 * C]
                        last = product(o, [(part(w1T_s, ALL, kk, cols(m)), part(gx, ALL, kk))
                                           for kk in range(KD)])
                        if m == 1:
                            last.then_inc(pe_R0, 1)
                    last.then_inc(pe_did["R"], 1)
                if first(n, 1):
                    for m in range(KH):
                        last = mm(psum[:, 3, 0:D], beta_b[:, m, :], w2T_f[m // 2][:, m % 2], m == 0, m == KH - 1)
                    last.then_inc(betaW_sums, 1)
                if active("G", n):
                    p = n
                    pe.wait_ge(bh_made, upto(p))
                    pe.wait_ge(w_lo, upto(p))
                    if begun(n - 5):
                        pe.wait_ge(ax3_lo, upto(n - 5))
                    for g in range(2):
                        o = psum[:, BANK["G"], g * (C + 2):(g + 1) * (C + 2)]
                        mm(o, HT[:, g, :], BH[:, 0, g, :], True, False)
                        last = mm(o, HT[:, g, :], BH[:, 1, g, :], False, True)
                    last.then_inc(pe_did["G"], 1)
                if active("xT", n):
                    p = n - 2
                    pe.wait_ge(n1.done, upto(p))
                    pe.wait_ge(p_made, upto(p))
                    for m in range(KD):
                        for g in range(2):
                            last = pe.transpose(psum[:, BANK["xT"], (2 * m + g) * C:(2 * m + g + 1) * C],
                                                x1[:, g, cols(m)], ident[:])
                    last.then_inc(pe_did["xT"], 1)
                if active("H2W", n):
                    p = n - 4
                    pe.wait_ge(h2_hi, upto(p))
                    pe.wait_ge(h2_lo, upto(p))
                    pe.wait_ge(h1w_out, upto(p))
                    weigh("H2W", h2_s, v_s[2])
                if active("Ax2", n):
                    p = n - 3
                    pe.wait_ge(n2.done, upto(p))
                    pe.wait_ge(a_copied, upto(p))
                    pe.wait_ge(r_relu[1], upto(n - 1))
                    propagate_T("Ax2", x2, A_f[(k - 3) % RING])
                if active("XAB", n):
                    p = n - 2
                    pe.wait_ge(x1T_hi, upto(p))
                    pe.wait_ge(x1T_lo, upto(p))
                    if begun(n - 4):
                        pe.wait_ge(h2_relu, upto(n - 4))
                    if begun(n - 5):
                        pe.wait_ge(tk_relu, upto(n - 5))
                    if first(n, 2):
                        pe.wait_ge(wab_lo, 2)
                        pe.wait_ge(betaW_made, 1)
                    for g in range(2):
                        last = product(psum[:, BANK["XAB"] + g, :],
                                       [(part(x1T, ALL, m, g), part(wab_s, ALL, m)) for m in range(KD)])
                    last.then_inc(pe_did["XAB"], 1)
                if active("H1", n):
                    p = n - 3
                    pe.wait_ge(ax2_hi, upto(p))
                    pe.wait_ge(ax2_lo, upto(p))
                    pe.wait_ge(r_relu[0], upto(n - 1))
                    if first(n, 3):
                        pe.wait_ge(v_lo, 4)
                    for m in range(KD):
                        last = product(psum[:, BANK["H1"], m * 2 * C:(m + 1) * 2 * C],
                                       [(part(v_s[0], ALL, kk, cols(m)), part(ax2, ALL, kk)) for kk in range(KD)])
                    last.then_inc(pe_did["H1"], 1)
                if active("AP3", n):
                    p = n - 4
                    pe.wait_ge(h2w_hi, upto(p))
                    pe.wait_ge(h2w_lo, upto(p))
                    pe.wait_ge(gd_made, upto(n))
                    for g in range(2):
                        last = product(psum[:, BANK["AP3"], g * D:(g + 1) * D],
                                       [(part(A[(k - 4) % RING], ALL, g), part(h2w, ALL, g))])
                    last.then_inc(pe_did["AP3"], 1)
                if active("P", n):
                    p = n - 1
                    pe.wait_ge(r_hi[1], upto(p))
                    pe.wait_ge(r_lo, upto(p))
                    pe.wait_ge(sq_sum, upto(p))
                    if first(n, 1):
                        pe.wait_ge(w2c_lo, 1)
                    if begun(n - 2):
                        pe.wait_ge(x1T_lo, upto(n - 2))
                        pe.wait_ge(p_made, upto(n - 2))
                    for g in range(2):
                        product(psum[:, BANK["P"] + g, 0:D + 2],
                                [(part(r_s, ALL, m, g), part(w2c_s, ALL, m)) for m in range(KH)])
                        last = mm(psum[:, BANK["P"] + g, D + 2:D + 3], sq1[:, g, :], ones[:, 0:1], True, True)
                    last.then_inc(pe_did["P"], 1)
                if active("Tr", n):
                    p = n
                    if first(n, 0):
                        pe.wait_ge(small_loaded, 16 * 3)
                    pe.wait_ge(gd_made, upto(p))
                    if begun(n - 3):
                        pe.wait_ge(ax2_lo, upto(n - 3))
                    for g in range(2):
                        last = pe.transpose(psum[:, BANK["Tr"], cols(g)], Gd[:, g, :], ident[:])
                    last.then_inc(pe_did["Tr"], 1)
                if active("AXB", n):
                    p = n - 2
                    pe.wait_ge(xbw_hi, upto(p))
                    pe.wait_ge(xbw_lo, upto(p))
                    pe.wait_ge(a_hi, upto(p))
                    pe.wait_ge(a_lo, upto(p))
                    for g in range(2):
                        last = product(psum[:, BANK["AXB"] + g, 0:D + 2],
                                       [(part(A[(k - 2) % RING], ALL, g), part(xbw, ALL, g))])
                    last.then_inc(pe_did["AXB"], 1)
                if active("H1W", n):
                    p = n - 3
                    pe.wait_ge(h1_hi, upto(p))
                    pe.wait_ge(h1_lo, upto(p))
                    if begun(n - 4):
                        pe.wait_ge(h2w_lo, upto(n - 4))
                    weigh("H1W", h1_s, v_s[1])
                if active("Ax3", n):
                    p = n - 4
                    pe.wait_ge(n3.done, upto(p))
                    propagate_T("Ax3", x3, A_f[(k - 4) % RING])
                if active("Gx", n):
                    p = n
                    pe.wait_ge(gt_made, upto(p))
                    pe.wait_ge(x_loaded[k % RING], at_count(p, k))
                    if begun(n - 3):
                        pe.wait_ge(h1_relu, upto(n - 3))
                    propagate_T("Gx", x_in[:, k % RING], GT[k % 2])
                if first(n, 0):
                    pe.wait_ge(w2_scaled, 2 * KH)
                    for m in range(KH):
                        last = mm(psum[:, 2, 0:D], ones[:], w2g[:, m, :], m == 0, m == KH - 1)
                    last.then_inc(w2_sums, 1)
                if active("GP", n):
                    p = n - 1
                    pe.wait_ge(p_made, upto(p))
                    pe.wait_ge(gt_made, upto(n))
                    for g in range(2):
                        last = mm(psum[:, BANK["GP"], g * D:(g + 1) * D], GT[(k - 1) % 2][:, g, :],
                                  p_f[:, g, :], True, True)
                    last.then_inc(pe_did["GP"], 1)
                if active("H2", n):
                    p = n - 3
                    pe.wait_ge(h1w_out, upto(p))
                    if begun(n - 2):
                        pe.wait_ge(agg_made, upto(n - 2))
                    propagate_T("H2", h1w, A_f[(k - 3) % RING])
                if active("TK", n):
                    p = n - 4
                    pe.wait_ge(ax3_hi, upto(p))
                    pe.wait_ge(ax3_lo, upto(p))
                    pe.wait_ge(agg_made, upto(n - 2))
                    weigh("TK", ax3, wk_s)

            steps(pe, body)

        @block.scalar
        def _(act):
            def copy(o, i):
                return act.activation(o, i, ACT.Copy)

            def split_hi(stage, dst, signal, p, used):
                act.wait_ge(pe_did[stage], upto(p))
                if begun(p - 1):
                    act.wait_ge(used, upto(p - 1))
                copy(dst[0][:].rearrange("p a b -> p (a b)") if len(dst[0].shape) == 3 else
                     dst[0][:].rearrange("p a b c -> p (a b c)"),
                     psum[:, BANK[stage], 0:2 * D]).then_inc(signal, 1)

            def root(nm, p):
                act.wait_ge(nm.varied, upto(p))
                if begun(p - 1):
                    act.wait_ge(nm.inverted, upto(p - 1))
                act.activation(nm.std[:], nm.mv[:, :, 1], ACT.Sqrt, bias=eps_c[:, 0:1]).then_inc(nm.rooted, 1)

            act.wait_ge(consts_step, 1)
            act.activation(h_std[:, 0:1], eps_c[:], ACT.Sqrt).then_inc(table_loaded, 1)
            act.wait_ge(table_loaded, 1)
            act.wait_ge(small_loaded, 16 * 3)
            act.wait_ge(consts_made, 1)
            act.wait_ge(w1_loaded, 16)
            copy(w1T_s[0][:], w1T_f).then_inc(w1_hi, 1)

            def relu_out(stage, m, dst, bias, extra=0):
                return act.activation(dst[:, m].rearrange("p g c -> p (g c)"),
                                      psum[:, BANK[stage] + extra, (m % 2) * 2 * C:(m % 2 + 1) * 2 * C],
                                      ACT.Relu, bias=bias[:, m:m + 1])

            def body(n, k):
                if first(n, 1):
                    act.wait_ge(wab_loaded, 16 * KD)
                    for kk in range(KD):
                        copy(wab_s[0][:, kk], wab_f[kk]).then_inc(wab_hi, 1)
                if first(n, 2):
                    act.wait_ge(v_lo, 4)
                    act.wait_ge(wab_lo, KD)
                if active("x2", n):
                    p = n - 3
                    act.wait_ge(n2.shifted, upto(p))
                    if begun(p - 1):
                        act.wait_ge(pe_did["Ax2"], upto(p - 1))
                        act.wait_ge(x2c_made, upto(p - 1))
                    for g in range(2):
                        last = act.activation(x2[:, g, :], n2.s[:, g, :], ACT.Identity,
                                              scale=n2.rstd[:, g:g + 1], bias=n2.shift[:, g:g + 1])
                    last.then_inc(n2.done, 1)
                if active("R", n):
                    p = n - 1
                    act.wait_ge(pe_R0, upto(p))
                    if begun(p - 1):
                        act.wait_ge(sq_made, upto(p - 1))
                        act.wait_ge(r_lo, upto(p - 1))
                    relu_out("R", 0, r_f, b1_c, 1)
                    relu_out("R", 1, r_f, b1_c, 1).then_inc(r_relu[0], 1)
                    act.wait_ge(pe_did["R"], upto(p))
                    relu_out("R", 2, r_f, b1_c)
                    relu_out("R", 3, r_f, b1_c).then_inc(r_relu[1], 1)
                if active("xT", n):
                    split_hi("xT", x1T, x1T_hi, n - 2, pe_did["XAB"])
                if active("R", n):
                    p = n - 1
                    act.wait_ge(r_relu[0], upto(p))
                    if begun(p - 1):
                        act.wait_ge(pe_did["P"], upto(p - 1))
                    copy(r_s[0][:, 0:2], r_f[:, 0:2]).then_inc(r_hi[0], 1)
                if active("H2W", n):
                    split_hi("H2W", h2w, h2w_hi, n - 4, pe_did["AP3"])
                if active("R", n):
                    act.wait_ge(r_relu[1], upto(n - 1))
                    copy(r_s[0][:, 2:4], r_f[:, 2:4]).then_inc(r_hi[1], 1)
                if active("Ax2", n):
                    split_hi("Ax2", ax2, ax2_hi, n - 3, pe_did["H1"])
                if active("R", n):
                    p = n - 1
                    if begun(p - 1):
                        act.wait_ge(sq_half, upto(p - 1))
                    act.activation(sq[:], r_f[:], ACT.Square).then_inc(sq_made, 1)
                    act.wait_ge(at_loaded[(k - 1) % RING], at_count(p, k - 1))
                    if begun(n - 5):
                        act.wait_ge(pe_did["Ax3"], upto(n - 5))
                    copy(A[(k - 1) % RING][0][:], at_in[:, (k - 1) % RING]).then_inc(a_hi, 1)
                    copy(A_f[(k - 1) % RING][:], at_in[:, (k - 1) % RING]).then_inc(a_copied, 1)
                if first(n, 1):
                    act.wait_ge(v_loaded, 16 * 4)
                    for dst, src in ((v_s[0], v_f[0]), (v_s[1], v_f[1]), (v_s[2], v_f[2]), (wk_s, wk_f)):
                        copy(dst[0][:], src).then_inc(v_hi, 1)
                if active("XAB", n):
                    p = n - 2
                    act.wait_ge(pe_did["XAB"], upto(p))
                    if begun(p - 1):
                        act.wait_ge(pe_did["AXB"], upto(p - 1))
                    b = BANK["XAB"]
                    copy(xbw[0][:, :, 0:D], psum[:, b:b + 2, D:2 * D]).then_inc(xbw_hi, 1)
                    if begun(p - 1):
                        act.wait_ge(agg_made, upto(p - 1))
                    copy(xa[:], psum[:, b:b + 2, 0:D]).then_inc(xa_out, 1)
                if active("H1", n):
                    p = n - 3
                    act.wait_ge(pe_did["H1"], upto(p))
                    if begun(p - 1):
                        act.wait_ge(h1_lo, upto(p - 1))
                    relu_out("H1", 0, h1_f, c1_c)
                    relu_out("H1", 1, h1_f, c1_c).then_inc(h1_relu, 1)
                    act.wait_ge(h1_relu, upto(p))
                    if begun(p - 1):
                        act.wait_ge(pe_did["H1W"], upto(p - 1))
                    copy(h1_s[0][:], h1_f[:]).then_inc(h1_hi, 1)
                if active("AP3", n):
                    root(n3, n - 4)
                if active("F", n):
                    root(n4, n - 5)
                if active("P", n):
                    b = BANK["P"]
                    act.wait_ge(pe_did["P"], upto(n - 1))
                    act.activation(h_mean2[:], psum[:, b:b + 2, D], ACT.Square, scale=1.0 / DH).then_inc(hm2, 1)
                if active("Tr", n):
                    p = n
                    act.wait_ge(pe_did["Tr"], upto(p))
                    if begun(p - 2):
                        act.wait_ge(pe_did["GP"], upto(p - 2))
                    copy(GT[k % 2][:].rearrange("p a b -> p (a b)"),
                         psum[:, BANK["Tr"], 0:2 * C]).then_inc(gt_made, 1)
                if active("P", n):
                    act.wait_ge(hve, upto(n - 1))
                    act.activation(h_std[:], h_veps[:], ACT.Sqrt).then_inc(hstd, 1)
                if active("H1W", n):
                    p = n - 3
                    act.wait_ge(pe_did["H1W"], upto(p))
                    if begun(p - 1):
                        act.wait_ge(pe_did["H2"], upto(p - 1))
                    copy(h1w[:].rearrange("p g d -> p (g d)"),
                         psum[:, BANK["H1W"], 0:2 * D]).then_inc(h1w_out, 1)
                if active("Ax3", n):
                    split_hi("Ax3", ax3, ax3_hi, n - 4, pe_did["TK"])
                if active("Gx", n):
                    split_hi("Gx", gx, gx_hi, n, pe_did["R"])
                if active("F", n):
                    p = n - 5
                    act.wait_ge(n4.shifted, upto(p))
                    if not isinstance(p, int):
                        act.wait_ge(stored[(k - 5) % 2], (p - (k - 5) % 2) * 8)
                    elif p >= 2:
                        act.wait_ge(stored[p % 2], 16 * (p // 2))
                    for g in range(2):
                        last = act.activation(x4[(k - 5) % 2][:, g, :], n4.s[:, g, :], ACT.Identity,
                                              scale=n4.rstd[:, g:g + 1], bias=n4.shift[:, g:g + 1])
                    last.then_inc(n4.done, 1)
                if active("H2", n):
                    p = n - 3
                    act.wait_ge(pe_did["H2"], upto(p))
                    if begun(p - 1):
                        act.wait_ge(h2_lo, upto(p - 1))
                    relu_out("H2", 0, h2_f, c2_c)
                    relu_out("H2", 1, h2_f, c2_c).then_inc(h2_relu, 1)
                if active("H2", n):
                    p = n - 3
                    act.wait_ge(h2_relu, upto(p))
                    if begun(p - 1):
                        act.wait_ge(pe_did["H2W"], upto(p - 1))
                    copy(h2_s[0][:], h2_f[:]).then_inc(h2_hi, 1)
                if active("AXB", n):
                    root(n2, n - 2)
                if active("TK", n):
                    p = n - 4
                    act.wait_ge(pe_did["TK"], upto(p))
                    if begun(p - 1):
                        act.wait_ge(tk_masked, upto(p - 1))
                    act.activation(tk[:].rearrange("p g d -> p (g d)"), psum[:, BANK["TK"], 0:2 * D],
                                   ACT.Relu).then_inc(tk_relu, 1)
                if active("GP", n):
                    root(n1, n - 1)

            steps(act, body)

        @block.vector
        def _(dve):
            def split_lo(dst, src, signal):
                return dve.tensor_tensor(dst[1][:], src, f(dst[0][:]), ALU.subtract).then_inc(signal, 1)

            dve.memset(ones[:], 1.0)
            dve.memset(eps_c[:], LN_EPS).then_inc(consts_step, 1)
            dve.wait_ge(consts_step, 1)
            pair01, four01 = ones[:, 0:2].unsqueeze(2), ones[:, 0:KH].unsqueeze(2)
            dve.tensor_copy(xbw[0][:, :, D:D + 1], pair01)
            dve.tensor_scalar(xbw[0][:, :, D + 1:D + 2], pair01, 0.0, None, ALU.mult)
            for h in range(2):
                dve.tensor_scalar(xbw[1][:, :, D + h:D + h + 1], pair01, 0.0, None, ALU.mult)
                dve.tensor_scalar(BH[:, h, :, C + 1:C + 2], pair01, 0.0, None, ALU.mult)
            dve.tensor_copy(w2c_s[0][:, :, D:D + 1], four01)
            dve.tensor_scalar(w2c_s[0][:, :, D + 1:D + 2], four01, 0.0, None, ALU.mult)
            for h in range(2):
                dve.tensor_scalar(w2c_s[1][:, :, D + h:D + h + 1], four01, 0.0, None, ALU.mult)
            dve.wait_ge(small_loaded, 16 * 3)
            dve.tensor_scalar(b2half[:], rows_b[:, 0], 0.5, None, ALU.mult).then_inc(consts_made, 1)

            def scale_w2():
                dve.wait_ge(w2_loaded, 16 * 2)
                for m in range(KH):
                    dve.tensor_scalar(w2g[:, m, :], w2T_f[m // 2][:, m % 2], gamma_c[:, m:m + 1], None,
                                      ALU.mult).then_inc(w2_scaled, 1)
                    dve.tensor_scalar(beta_b[:, m, :], ones[:], beta_c[:, m:m + 1], None,
                                      ALU.mult).then_inc(w2_scaled, 1)

            def centre_w2():
                dve.wait_ge(w2_sums, 1)
                dve.tensor_scalar(w2mean[:], psum[:, 2, 0:D], 1.0 / DH, None, ALU.mult).then_inc(w2_mean, 1)
                dve.wait_ge(w2_mean, 1)
                dve.wait_ge(w2_scaled, 2 * KH)
                dve.tensor_tensor(w2g[:], w2g[:], bc(w2mean[:], [C, KH, D], 1), ALU.subtract).then_inc(w2_centred, 1)
                dve.wait_ge(w2_centred, 1)
                dve.tensor_copy(w2c_s[0][:, :, 0:D], w2g[:]).then_inc(w2c_hi, 1)
                dve.wait_ge(w2c_hi, 1)
                dve.tensor_tensor(w2c_s[1][:, :, 0:D], w2g[:], f(w2c_s[0][:, :, 0:D]),
                                  ALU.subtract).then_inc(w2c_lo, 1)
                dve.wait_ge(wab_hi, KD)
                for kk in range(KD):
                    dve.tensor_tensor(wab_s[1][:, kk], wab_f[kk], f(wab_s[0][:, kk]),
                                      ALU.subtract).then_inc(wab_lo, 1)
                dve.wait_ge(betaW_sums, 1)
                dve.tensor_copy(betaW[:], psum[:, 3, 0:D]).then_inc(betaW_made, 1)

            def stats(nm, p):
                dve.wait_ge(nm.summed, upto(p))
                for g in range(2):
                    last = dve.bn_stats(nm.st[:, g, :], nm.s[:, g, :])
                last.then_inc(nm.stats, 1)

            def mean_var(nm):
                for g in range(2):
                    last = dve.bn_aggr(nm.mv[:, g, :], nm.st[:, g, :])
                last.then_inc(nm.varied, 1)

            def invert(nm, p):
                dve.wait_ge(nm.rooted, upto(p))
                if begun(p - 1):
                    dve.wait_ge(nm.done, upto(p - 1))
                dve.reciprocal(nm.rstd[:], nm.std[:]).then_inc(nm.inverted, 1)

            def shift(nm, p):
                dve.wait_ge(nm.inverted, upto(p))
                dve.scalar_tensor_tensor(out=nm.shift[:], in0=nm.mv[:, :, 0], scalar=-1.0, in1=nm.rstd[:],
                                         op0=ALU.mult, op1=ALU.mult).then_inc(nm.shifted, 1)

            def apply(nm, p, dst):
                dve.wait_ge(nm.inverted, upto(p))
                for g in range(2):
                    last = dve.tensor_scalar(dst[:, g, :], nm.s[:, g, :], nm.mv[:, g, 0:1], nm.rstd[:, g:g + 1],
                                             ALU.subtract, ALU.mult)
                last.then_inc(nm.done, 1)

            def flat(b):
                return psum[:, b, 0:2 * D]

            def body(n, k):
                if first(n, 1):
                    centre_w2()
                if first(n, 2):
                    dve.wait_ge(v_lo, 4)
                    dve.wait_ge(betaW_made, 1)
                if active("x1", n):
                    p = n - 2
                    invert(n1, p)
                    if begun(p - 1):
                        dve.wait_ge(pe_did["xT"], upto(p - 1))
                    apply(n1, p, x1)
                if active("F", n):
                    p = n - 5
                    dve.wait_ge(n3.done, upto(p))
                    if begun(p - 1):
                        dve.wait_ge(n4.summed, upto(p - 1))
                    for g in range(2):
                        last = dve.tensor_scalar(nz[:, g, :], x3[:, g, :], 0.0, 0.0, ALU.not_equal, ALU.add,
                                                 accum_out=nz_count[:, g:g + 1])
                    last.then_inc(x3_nz, 1)
                    dve.wait_ge(x3_nz, upto(p))
                    dve.tensor_scalar(mask[:], nz_count[:], 0.0, None, ALU.is_gt).then_inc(mask_made, 1)
                if active("xT", n):
                    dve.wait_ge(x1T_hi, upto(n - 2))
                    split_lo(x1T, flat(BANK["xT"]), x1T_lo)
                if active("H2W", n):
                    dve.wait_ge(h2w_hi, upto(n - 4))
                    split_lo(h2w, flat(BANK["H2W"]), h2w_lo)
                if active("Ax2", n):
                    dve.wait_ge(ax2_hi, upto(n - 3))
                    split_lo(ax2, flat(BANK["Ax2"]), ax2_lo)

                q = n + 1
                g_dn = psum[:, BANK["G"], 0:2 * (C + 2)].rearrange("p (g c) -> p g c", g=2)
                dn = g_dn[:, :, C]
                w = at_in[:, (k + 1) % RING, :, 0:1]
                if active("G", n):
                    dve.wait_ge(pe_did["G"], upto(n))
                    dve.tensor_scalar(dn_max[:], dn, TINY, None, ALU.max).then_inc(dn_1, 1)
                if active("prep", n):
                    dve.wait_ge(at_loaded[(k + 1) % RING], at_count(q, k + 1))
                    if begun(n):
                        dve.wait_ge(pe_did["G"], upto(n))
                    dve.tensor_scalar(HT[:], at_in[:, (k + 1) % RING], 0.0, None,
                                      ALU.not_equal).then_inc(ht_made, 1)
                if active("G", n):
                    dve.wait_ge(dn_1, upto(n))
                    dve.reciprocal(dn_inv[:], dn_max[:]).then_inc(dn_2, 1)
                if active("prep", n):
                    dve.wait_ge(ht_made, upto(q))
                    dve.tensor_reduce(ht_count[:], f(HT[:]), AX_X, ALU.add).then_inc(ht_counted, 1)
                if active("G", n):
                    dve.wait_ge(dn_2, upto(n))
                    dve.scalar_tensor_tensor(out=dinv[:], in0=dn, scalar=0.0, in1=dn_inv[:],
                                             op0=ALU.is_gt, op1=ALU.mult).then_inc(dn_3, 1)
                if active("prep", n):
                    dve.tensor_copy(BH[:, 0, :, C:C + 1], w).then_inc(w_hi, 1)
                    dve.wait_ge(ht_counted, upto(q))
                    dve.tensor_scalar(be[:], ht_count[:], 1.0, None, ALU.max).then_inc(be_max, 1)
                if active("G", n):
                    dve.wait_ge(dn_3, upto(n))
                    if begun(n - 1):
                        dve.wait_ge(pe_did["Tr"], upto(n - 1))
                    dve.tensor_tensor(Gd[:], g_dn[:, :, 0:C], bc(dinv[:], [C, 2, C], 2),
                                      ALU.mult).then_inc(gd_made, 1)
                if active("prep", n):
                    dve.wait_ge(be_max, upto(q))
                    if begun(q - 1):
                        dve.wait_ge(bh_made, upto(q - 1))
                    dve.reciprocal(be_parts[:, 1, :], be[:]).then_inc(be_made, 1)
                    dve.wait_ge(w_hi, upto(q))
                    dve.tensor_tensor(BH[:, 1, :, C:C + 1], w, f(BH[:, 0, :, C:C + 1]),
                                      ALU.subtract).then_inc(w_lo, 1)
                    dve.wait_ge(be_made, upto(q))
                    dve.tensor_copy(be_r[:], be_parts[:, 1, :]).then_inc(be_hi, 1)
                    dve.wait_ge(be_hi, upto(q))
                    dve.tensor_copy(be_parts[:, 0, :], f(be_r[:]))
                    dve.tensor_tensor(be_parts[:, 1, :], be_parts[:, 1, :], f(be_r[:]),
                                      ALU.subtract).then_inc(be_lo, 1)

                if first(n, 0):
                    scale_w2()
                if active("AP3", n):
                    p = n - 4
                    dve.wait_ge(pe_did["AP3"], upto(p))
                    dve.wait_ge(x2c_made, upto(p))
                    dve.tensor_tensor(n3.s[:].rearrange("p g d -> p (g d)"), flat(BANK["AP3"]),
                                      x2c[(k - 4) % 2][:].rearrange("p g d -> p (g d)"),
                                      ALU.add).then_inc(n3.summed, 1)
                    stats(n3, p)
                if active("XAB", n):
                    p = n - 2
                    dve.wait_ge(xbw_hi, upto(p))
                    dve.wait_ge(xa_out, upto(p))
                    if active("AP3", n):
                        dve.wait_ge(n3.stats, upto(n - 4))
                    dve.tensor_tensor(xbw[1][:, :, 0:D], psum[:, BANK["XAB"]:BANK["XAB"] + 2, D:2 * D],
                                      f(xbw[0][:, :, 0:D]), ALU.subtract).then_inc(xbw_lo, 1)
                elif active("AP3", n):
                    dve.wait_ge(n3.stats, upto(n - 4))
                    dve.memset(wait_pad[:], 0.0)
                if active("AP3", n):
                    mean_var(n3)
                if active("F", n):
                    stats(n4, n - 5)
                if active("AP3", n):
                    p = n - 4
                    invert(n3, p)
                if active("F", n):
                    dve.wait_ge(n4.stats, upto(n - 5))
                    dve.memset(wait_pad[:], 0.0)
                    mean_var(n4)
                b = BANK["P"]
                if active("AP3", n):
                    p = n - 4
                    if begun(p - 1):
                        dve.wait_ge(pe_did["Ax3"], upto(p - 1))
                        dve.wait_ge(n4.summed, upto(p - 1))
                    apply(n3, p, x3)
                if active("P", n):
                    dve.wait_ge(hm2, upto(n - 1))
                    dve.scalar_tensor_tensor(out=h_var[:], in0=psum[:, b:b + 2, D + 2], scalar=1.0 / DH,
                                             in1=h_mean2[:], op0=ALU.mult, op1=ALU.subtract).then_inc(hv, 1)
                    dve.wait_ge(hv, upto(n - 1))
                    dve.tensor_scalar(h_veps[:], h_var[:], 0.0, LN_EPS, ALU.max, ALU.add).then_inc(hve, 1)
                if active("AXB", n):
                    dve.wait_ge(pe_did["AXB"], upto(n - 2))
                    dve.tensor_scalar(degm[:], psum[:, BANK["AXB"]:BANK["AXB"] + 2, D], DEG_EPS, None,
                                      ALU.max).then_inc(deg_max, 1)
                if active("F", n):
                    invert(n4, n - 5)
                if active("P", n):
                    dve.wait_ge(hstd, upto(n - 1))
                    dve.reciprocal(h_rstd[:], h_std[:]).then_inc(hrstd, 1)
                if active("AXB", n):
                    dve.wait_ge(deg_max, upto(n - 2))
                    dve.reciprocal(rdeg[:], degm[:]).then_inc(deg_inv, 1)
                if active("F", n):
                    shift(n4, n - 5)
                if active("P", n):
                    p = n - 1
                    dve.wait_ge(hrstd, upto(p))
                    if begun(p - 1):
                        dve.wait_ge(pe_did["GP"], upto(p - 1))
                    for g in range(2):
                        last = dve.scalar_tensor_tensor(out=p_f[:, g, :], in0=psum[:, b + g, 0:D],
                                                        scalar=h_rstd[:, g:g + 1], in1=betaW[:],
                                                        op0=ALU.mult, op1=ALU.add)
                    last.then_inc(p_made, 1)

                if active("AXB", n):
                    p = n - 2
                    dve.wait_ge(xa_out, upto(p))
                    dve.wait_ge(deg_inv, upto(p))
                    for g in range(2):
                        last = dve.scalar_tensor_tensor(out=agg[:, g, :], in0=psum[:, BANK["AXB"] + g, 0:D],
                                                        scalar=rdeg[:, g:g + 1],
                                                        in1=xa[:, g, :], op0=ALU.mult, op1=ALU.add)
                    last.then_inc(agg_made, 1)
                if active("Ax3", n):
                    dve.wait_ge(ax3_hi, upto(n - 4))
                    split_lo(ax3, flat(BANK["Ax3"]), ax3_lo)
                if active("AXB", n):
                    p = n - 2
                    dve.wait_ge(agg_made, upto(p))
                    if begun(p - 1):
                        dve.wait_ge(n2.done, upto(p - 1))
                    dve.scalar_tensor_tensor(out=n2.s[:], in0=agg[:], scalar=0.0, in1=x1[:],
                                             op0=ALU.max, op1=ALU.add).then_inc(n2.summed, 1)
                if active("Gx", n):
                    dve.wait_ge(gx_hi, upto(n))
                    split_lo(gx, flat(BANK["Gx"]), gx_lo)
                if active("GP", n):
                    p = n - 1
                    dve.wait_ge(pe_did["GP"], upto(p))
                    dve.wait_ge(xb_made, upto(p))
                    dve.scalar_tensor_tensor(out=n1.s[:].rearrange("p g d -> p (g d)"),
                                             in0=xb[:].rearrange("p g d -> p (g d)"), scalar=2.0,
                                             in1=flat(BANK["GP"]), op0=ALU.mult,
                                             op1=ALU.add).then_inc(n1.summed, 1)
                if active("AXB", n):
                    stats(n2, n - 2)
                    dve.wait_ge(n2.stats, upto(n - 2))
                    dve.memset(wait_pad[:], 0.0)
                    mean_var(n2)
                if active("GP", n):
                    stats(n1, n - 1)
                if active("AXB", n):
                    if active("GP", n):
                        dve.wait_ge(n1.stats, upto(n - 1))
                    invert(n2, n - 2)
                elif active("GP", n):
                    dve.wait_ge(n1.stats, upto(n - 1))
                    dve.memset(wait_pad[:], 0.0)
                if active("GP", n):
                    mean_var(n1)
                if active("AXB", n):
                    shift(n2, n - 2)

            steps(dve, body)

        @block.gpsimd
        def _(pool):
            def lo(dst, src, signal):
                return pool.tensor_tensor(dst[1][:], src, f(dst[0][:]), ALU.subtract).then_inc(signal, 1)

            pool.wait_ge(consts_made, 1)

            def body(n, k):
                if first(n, 0):
                    pool.wait_ge(w1_loaded, 16)
                    pool.wait_ge(w1_hi, 1)
                    lo(w1T_s, w1T_f, w1_lo)
                if active("F", n):
                    p = n - 5
                    pool.wait_ge(tk_relu, upto(p))
                    pool.wait_ge(mask_made, upto(p))
                    if begun(p - 1):
                        pool.wait_ge(n4.done, upto(p - 1))
                    pool.tensor_tensor(n4.s[:], tk[:], bc(mask[:], [C, 2, D], 2), ALU.mult).then_inc(tk_masked, 1)
                if active("R", n):
                    p = n - 1
                    pool.wait_ge(r_hi[0], upto(p))
                    if begun(p - 1):
                        pool.wait_ge(pe_did["P"], upto(p - 1))
                    pool.tensor_tensor(r_s[1][:, 0:2], r_f[:, 0:2], f(r_s[0][:, 0:2]), ALU.subtract)
                    pool.wait_ge(r_hi[1], upto(p))
                    pool.tensor_tensor(r_s[1][:, 2:4], r_f[:, 2:4], f(r_s[0][:, 2:4]),
                                       ALU.subtract).then_inc(r_lo, 1)
                    pool.wait_ge(sq_made, upto(p))
                    pool.tensor_tensor(sq2[:], sq[:, 0:2], sq[:, 2:4], ALU.add).then_inc(sq_half, 1)
                    pool.wait_ge(sq_half, upto(p))
                    pool.tensor_tensor(sq1[:], sq2[:, 0], sq2[:, 1], ALU.add).then_inc(sq_sum, 1)
                    pool.wait_ge(a_hi, upto(p))
                    lo(A[(k - 1) % RING], at_in[:, (k - 1) % RING], a_lo)
                if active("F", n):
                    pool.wait_ge(tk_masked, upto(n - 5))
                    pool.tensor_tensor(n4.s[:], n4.s[:], x3[:], ALU.add).then_inc(n4.summed, 1)
                if active("H1", n):
                    pool.wait_ge(h1_hi, upto(n - 3))
                    lo(h1_s, h1_f[:], h1_lo)
                if active("prep", n):
                    q = n + 1
                    pool.wait_ge(be_lo, upto(q))
                    if begun(n):
                        pool.wait_ge(pe_did["G"], upto(n))
                    for h in range(2):
                        last = pool.tensor_tensor(BH[:, h, :, 0:C], f(HT[:]), bc(be_parts[:, h, :], [C, 2, C], 2),
                                                  ALU.mult)
                    last.then_inc(bh_made, 1)
                if first(n, 1):
                    pool.wait_ge(v_hi, 4)
                    for dst, src in ((v_s[0], v_f[0]), (v_s[1], v_f[1]), (v_s[2], v_f[2]), (wk_s, wk_f)):
                        lo(dst, src, v_lo)
                if active("x2", n):
                    p = n - 3
                    pool.wait_ge(n2.done, upto(p))
                    if begun(p - 2):
                        pool.wait_ge(n3.summed, upto(p - 2))
                    pool.tensor_tensor(x2c[(k - 3) % 2][:], x2[:], bc(c3_b, [C, 2, D], 1),
                                       ALU.add).then_inc(x2c_made, 1)
                if active("GP", n):
                    p = n - 1
                    if begun(p - 1):
                        pool.wait_ge(n1.summed, upto(p - 1))
                    pool.tensor_tensor(xb[:], x_in[:, (k - 1) % RING], bc(b2half[:], [C, 2, D], 1),
                                       ALU.add).then_inc(xb_made, 1)
                if active("H2", n):
                    pool.wait_ge(h2_hi, upto(n - 3))
                    lo(h2_s, h2_f[:], h2_lo)

            steps(pool, body)


def kernel(x, adj, L0_gnn_W1, L0_gnn_b1, L0_gnn_gamma, L0_gnn_beta, L0_gnn_W2, L0_gnn_b2, L1_gnn_W,
           L2_gnn_W1, L2_gnn_b1, L2_gnn_W2, L2_gnn_b2, L2_gnn_W3, L2_gnn_b3, L3_gnn_kernel):
    import numpy as np
    import concourse.bacc as bacc
    from concourse.bass_utils import run_bass_kernel_spmd

    x, adj = np.asarray(x), np.asarray(adj)
    N, C, D = x.shape

    def chunks(w):
        w = np.asarray(w)
        return np.ascontiguousarray(w.reshape(w.shape[0] // C, C, w.shape[1]).transpose(1, 0, 2))

    def column(v):
        return np.ascontiguousarray(np.asarray(v).reshape(-1, C).T)

    arrays = {
        "x_in_dram": np.ascontiguousarray(x.reshape(N // 2, 2, C, D).transpose(0, 2, 1, 3)),
        "adjT": np.ascontiguousarray(adj.reshape(N // 2, 2, C, C).transpose(0, 3, 1, 2)),
        "w1T_in": chunks(np.asarray(L0_gnn_W1).T), "w2T_in": chunks(np.asarray(L0_gnn_W2).T),
        "wab_in": np.ascontiguousarray(np.asarray(L1_gnn_W).T.reshape(2, D // C, C, D).transpose(2, 1, 0, 3)
                                       .reshape(C, D // C, 2 * D)),
        "v1_in": chunks(L2_gnn_W1), "v2_in": chunks(L2_gnn_W2), "v3_in": chunks(L2_gnn_W3),
        "wk_in": chunks(L3_gnn_kernel),
        "columns_in": np.concatenate([column(v) for v in (L0_gnn_gamma, L0_gnn_beta, L0_gnn_b1,
                                                          L2_gnn_b1, L2_gnn_b2)], axis=1),
        "rows_in": np.stack([np.asarray(L0_gnn_b2), np.asarray(L2_gnn_b3)]),
        "eye": np.eye(C, dtype=np.float32),
    }
    nc = bacc.Bacc("TRN2", target_bir_lowering=False, num_devices=1)
    args = [nc.dram_tensor(name, a.shape, mybir.dt.from_np(a.dtype), kind="ExternalInput").ap()
            for name, a in arrays.items()]
    out = nc.dram_tensor("out", (N // 2, C, 2, D), F32, kind="ExternalOutput").ap()
    build(nc, *args, out)
    r = run_bass_kernel_spmd(nc, [arrays], core_ids=[0])
    got = r.results[0]["out"]
    return np.ascontiguousarray(got.transpose(0, 2, 1, 3)).reshape(N, C, D)
```
